# Optimizing a Trainium2 kernel written in Bass

```python
import numpy as np
import jax
import jax.numpy as jnp

def _softmax(x, axis=-1):
    return jax.nn.softmax(x, axis=axis)

def _gelu(x):
    return jax.nn.gelu(x, approximate=True)

def _silu(x):
    return jax.nn.silu(x)

def _sigmoid(x):
    return jax.nn.sigmoid(x)

def _layernorm(x, axis=-1, eps=1e-05):
    m = jnp.mean(x, axis=axis, keepdims=True)
    v = jnp.var(x, axis=axis, keepdims=True)
    return (x - m) / jnp.sqrt(v + eps)

def _scatter_add(tgt, idx, src, axis=0):
    return tgt.at[idx].add(src)

def _segment_sum(src, seg, n):
    return jax.ops.segment_sum(src, seg, n)
kernel_name = 'mk_adj_preln_d2_adj_r2_8a39d0'

def setup_inputs(seed: int=0):
    np.random.seed(seed)
    _w = jnp.asarray

    def _rec_inputs():
        import jax
        import jax.numpy as jnp
        _gk = jax.random.key(seed)
        x = -0.0002928 + 1 * jax.random.normal(jax.random.fold_in(_gk, 1), (32, 256, 256), jnp.float32)
        _a = jax.random.bernoulli(jax.random.fold_in(_gk, 2), 0.0625, (32, 256, 256))
        _a = jnp.logical_or(_a, jnp.swapaxes(_a, -1, -2))
        _a = jnp.logical_or(_a, jnp.eye(256, dtype=bool))
        adj = _a.astype(jnp.int32)
        return (x, adj)
    x, adj = _rec_inputs()

    def _L0_gnn_setup():
        import jax, jax.numpy as jnp
        import numpy as np
        L = 3
        D = 256
        B, N = (8, 512)
        EPS = 1e-05

        def layernorm(x, gamma, beta):
            mu = jnp.mean(x, axis=-1, keepdims=True)
            var = jnp.var(x, axis=-1, keepdims=True)
            return (x - mu) * jax.lax.rsqrt(var + EPS) * gamma + beta
        key = jax.random.key(seed)
        ks = jax.random.split(key, 12)
        s = 1.0 / np.sqrt(D)
        node_features = jax.random.normal(ks[0], (B, N, D), dtype=jnp.float32)
        adjacency_matrix = jax.random.randint(ks[1], (B, N, N), 0, 2, dtype=jnp.int32)
        return {'node_features': node_features, 'adjacency_matrix': adjacency_matrix, 'attn_w': jax.random.normal(ks[2], (L, 2 * D), dtype=jnp.float32) * (1.0 / np.sqrt(2 * D)), 'attn_b': jax.random.normal(ks[3], (L,), dtype=jnp.float32) * 0.01, 'W1': jax.random.normal(ks[4], (L, D, 4 * D), dtype=jnp.float32) * s, 'b1': jnp.zeros((L, 4 * D), dtype=jnp.float32), 'W2': jax.random.normal(ks[5], (L, 4 * D, D), dtype=jnp.float32) * (1.0 / np.sqrt(4 * D)), 'b2': jnp.zeros((L, D), dtype=jnp.float32), 'g1': jnp.ones((L, D), dtype=jnp.float32), 'beta1': jnp.zeros((L, D), dtype=jnp.float32), 'g2': jnp.ones((L, D), dtype=jnp.float32), 'beta2': jnp.zeros((L, D), dtype=jnp.float32)}
    _L0_gnn_all = _L0_gnn_setup()
    _L0_gnn_in = {k: v for k, v in _L0_gnn_all.items() if k in ('attn_w', 'attn_b', 'W1', 'b1', 'W2', 'b2', 'g1', 'beta1', 'g2', 'beta2')}
    del _L0_gnn_all

    def _L1_gnn_setup():
        import jax, jax.numpy as jnp
        import numpy as np
        ALPHA = 0.2
        K_NUM = 16
        NEG_INF = -9000000000000000.0
        key = jax.random.key(seed)
        k1, k2, k3, k4 = jax.random.split(key, 4)
        B, N, F_in, F_out = (4, 1024, 256, 256)
        h = jax.random.normal(k1, (B, N, F_in), dtype=jnp.float32)
        adj = jax.random.randint(k2, (B, N, N), 0, 2, dtype=jnp.int32)

        def xavier(k, shape, gain=1.414):
            fan_in, fan_out = (shape[0], shape[1])
            bound = gain * np.sqrt(6.0 / (fan_in + fan_out))
            return jax.random.uniform(k, shape, jnp.float32, -bound, bound)
        W = xavier(k3, (F_in, F_out))
        a = xavier(k4, (2 * F_out, 1))
        return {'h': h, 'adj': adj, 'W': W, 'a': a}
    _L1_gnn_all = _L1_gnn_setup()
    _L1_gnn_in = {k: v for k, v in _L1_gnn_all.items() if k in ('W', 'a')}
    del _L1_gnn_all
    return {'x': x, 'adj': adj, 'L0_gnn_attn_w': _L0_gnn_in['attn_w'], 'L0_gnn_attn_b': _L0_gnn_in['attn_b'], 'L0_gnn_W1': _L0_gnn_in['W1'], 'L0_gnn_b1': _L0_gnn_in['b1'], 'L0_gnn_W2': _L0_gnn_in['W2'], 'L0_gnn_b2': _L0_gnn_in['b2'], 'L0_gnn_g1': _L0_gnn_in['g1'], 'L0_gnn_beta1': _L0_gnn_in['beta1'], 'L0_gnn_g2': _L0_gnn_in['g2'], 'L0_gnn_beta2': _L0_gnn_in['beta2'], 'L1_gnn_W': _L1_gnn_in['W'], 'L1_gnn_a': _L1_gnn_in['a']}

def reference(x, adj, L0_gnn_attn_w, L0_gnn_attn_b, L0_gnn_W1, L0_gnn_b1, L0_gnn_W2, L0_gnn_b2, L0_gnn_g1, L0_gnn_beta1, L0_gnn_g2, L0_gnn_beta2, L1_gnn_W, L1_gnn_a):
    import jax
    import jax.numpy as jnp

    def _L0_gnn_ref(node_features, adjacency_matrix, attn_w, attn_b, W1, b1, W2, b2, g1, beta1, g2, beta2):
        import jax, jax.numpy as jnp
        import numpy as np
        L = 3
        D = 256
        B, N = (8, 512)
        EPS = 1e-05

        def layernorm(x, gamma, beta):
            mu = jnp.mean(x, axis=-1, keepdims=True)
            var = jnp.var(x, axis=-1, keepdims=True)
            return (x - mu) * jax.lax.rsqrt(var + EPS) * gamma + beta
        n = adjacency_matrix.shape[-1]
        mask = adjacency_matrix.astype(jnp.float32) + jnp.eye(n, dtype=jnp.float32) > 0
        x = node_features
        d = x.shape[-1]
        for l in range(attn_w.shape[0]):
            si = x @ attn_w[l, :d]
            sj = x @ attn_w[l, d:]
            scores = si[:, :, None] + sj[:, None, :] + attn_b[l]
            scores = jnp.where(scores >= 0, scores, 0.2 * scores)
            scores = jnp.where(mask, scores, -jnp.inf)
            attn = jax.nn.softmax(scores, axis=-1)
            agg = jnp.einsum('bij,bjd->bid', attn, x)
            h = layernorm(x + agg, g1[l], beta1[l])
            ff = jax.nn.gelu(h @ W1[l] + b1[l], approximate=False) @ W2[l] + b2[l]
            x = layernorm(h + ff, g2[l], beta2[l])
        return x

    def _L1_gnn_ref(h, adj, W, a):
        import jax, jax.numpy as jnp
        import numpy as np
        ALPHA = 0.2
        K_NUM = 16
        NEG_INF = -9000000000000000.0
        F_out = W.shape[1]
        Wh = jnp.einsum('bnf,fo->bno', h, W)
        a1, a2 = (a[:F_out, 0], a[F_out:, 0])
        e_src = Wh @ a1
        e_dst = Wh @ a2
        e = e_src[:, :, None] + e_dst[:, None, :]
        e = jnp.where(e > 0, e, ALPHA * e)
        e = jnp.where(adj > 0, e, NEG_INF)
        attention = jax.nn.softmax(e, axis=2)
        topk_vals = jax.lax.top_k(attention, K_NUM)[0]
        kth = topk_vals[:, :, -1:]
        attention = jnp.where(attention < kth, 0.0, attention)
        h_prime = jnp.einsum('bij,bjo->bio', attention, Wh)
        return jax.nn.elu(h_prime)
    h = jnp.maximum(_layernorm(x, axis=-1), 0.0)
    x = x + _L0_gnn_ref(h, adj, L0_gnn_attn_w, L0_gnn_attn_b, L0_gnn_W1, L0_gnn_b1, L0_gnn_W2, L0_gnn_b2, L0_gnn_g1, L0_gnn_beta1, L0_gnn_g2, L0_gnn_beta2)
    h = jnp.maximum(_layernorm(x, axis=-1), 0.0)
    x = x + _L1_gnn_ref(h, adj, L1_gnn_W, L1_gnn_a)
    return x

_drawn_inputs = setup_inputs


def setup_inputs(seed=0):
    import zlib

    import numpy as np

    out = dict(_drawn_inputs(seed))
    spreads = {'L0_gnn_b1': (0.0, 0.1),
     'L0_gnn_b2': (0.0, 0.1),
     'L0_gnn_g1': (1.0, 0.2),
     'L0_gnn_beta1': (0.0, 0.1),
     'L0_gnn_g2': (1.0, 0.2),
     'L0_gnn_beta2': (0.0, 0.1)}
    factors = {'L0_gnn_attn_b': 180.025}
    for name, (base, spread) in spreads.items():
        noise = np.random.default_rng([zlib.crc32(name.encode()), seed]).standard_normal(out[name].shape)
        drawn = base * np.exp(spread * noise) if base else spread * noise
        out[name] = jnp.asarray(drawn.astype(out[name].dtype))
    for name, factor in factors.items():
        out[name] = (out[name] * factor).astype(out[name].dtype)
    return out
```

```python
import concourse.bass as bass
from concourse import mybir
from contextlib import ExitStack


def gnn_adjacency_kernel(nc, x, adj, vectors, attn_b, w1, b1, w2, w_out, a_out, neg_mask, out):
    F32 = mybir.dt.float32
    F32R = mybir.dt.float32r
    BF16 = mybir.dt.bfloat16
    I32 = mybir.dt.int32
    ALU = mybir.AluOpType
    ACT = mybir.ActivationFunctionType
    AX = mybir.AxisListType

    P = 128
    BATCH, N, D = x.shape
    LAYERS, HIDDEN = w1.shape[0], w1.shape[2]
    GRAPHS = 2
    GROUPS = BATCH // GRAPHS
    NB = N // P
    KB = D // P
    TILES = GRAPHS * NB
    FB = HIDDEN // P
    TOK = TILES * P
    UNITS = LAYERS * GROUPS
    EPS = 1e-5
    SLOPE = 0.2
    TOP = 16
    DMA = 16
    VEC = ("w_src", "w_dst", "gamma1", "beta1", "b2", "gamma2", "beta2")
    NV = len(VEC)

    x_rows = x.rearrange("b n d -> (b n) d")
    adj_rows = adj.rearrange("b n d -> (b n) d")
    out_rows = out.rearrange("b n d -> (b n) d")

    def dram_group(rows, g):
        return rows[bass.ds(g * TOK, TOK), :].rearrange("(c p) d -> p c d", p=P)

    ctx = ExitStack()
    with ctx:
        def sb(name, shape, dt):
            return ctx.enter_context(nc.sbuf_tensor(name, shape, dt))

        def sem(name):
            return ctx.enter_context(nc.semaphore(name))

        state = sb("state", [P, GROUPS, TILES, D], F32)
        w1_hi = sb("w1_hi", [P, KB, HIDDEN], F32R)
        w1_lo = sb("w1_lo", [P, KB, HIDDEN], F32R)
        w2_hi = sb("w2_hi", [P, FB, D], F32R)
        w2_lo = sb("w2_lo", [P, FB, D], F32R)
        w_raw = sb("w_raw", [P, 2, 1024], F32)
        vec = sb("vec", [P, LAYERS, NV, D], F32)
        mask = sb("mask", [P, 2, TILES, N], BF16)
        prob = sb("prob", [P, TILES, N], F32)
        x_hi = sb("x_hi", [P, TILES, D], F32R)
        x_lo = sb("x_lo", [P, TILES, D], F32R)
        pt_hi = sb("pt_hi", [P, GRAPHS, NB, N], F32R)
        pt_lo = sb("pt_lo", [P, GRAPHS, NB, N], F32R)
        h = sb("h", [P, TILES, D], F32)
        h_bias = sb("h_bias", [P, 2, TILES, D], F32)
        ht_hi = sb("ht_hi", [P, KB, TOK], F32R)
        ht_lo = sb("ht_lo", [P, KB, TOK], F32R)
        g_raw = sb("g_raw", [P, 2, TOK], F32)
        gt_hi = sb("gt_hi", [P, FB, TOK], F32R)
        gt_lo = sb("gt_lo", [P, FB, TOK], F32R)
        ident = sb("ident", [P, P], F32)
        ident_r = sb("ident_r", [P, P], F32R)
        neg_diag = sb("neg_diag", [P, P], BF16)
        b1_col = sb("b1_col", [P, LAYERS * FB], F32)
        ab_col = sb("ab_col", [P, LAYERS], F32)
        src_dst = sb("src_dst", [P, 2, TILES], F32)
        src_b = sb("src_b", [P, TILES], F32)
        dst_hi = sb("dst_hi", [P, TILES], F32R)
        dst_lo = sb("dst_lo", [P, TILES], F32R)
        neg_max = sb("neg_max", [P, TILES], F32)
        row_sum = sb("row_sum", [P, TILES], F32)
        row_inv = sb("row_inv", [P, TILES], F32)
        stats = sb("stats", [P, TILES, 6], F32)
        mean_var = sb("mean_var", [P, TILES, 2], F32)
        var_eps = sb("var_eps", [P, TILES], F32)
        rstd = sb("rstd", [P, TILES], F32)
        minus_half = sb("minus_half", [P, TILES], F32)
        top8 = sb("top8", [P, TILES, 8], F32)
        next8 = sb("next8", [P, TILES, 8], F32)

        mask_dram = nc.dram_tensor("mask_store", [GROUPS, P, TILES * N], BF16, kind="Internal").ap()

        z_ps = ctx.enter_context(nc.psum_tensor("z_ps", [P, 2, TOK], F32))
        y_ps = ctx.enter_context(nc.psum_tensor("y_ps", [P, TILES, D], F32))
        s_ps = ctx.enter_context(nc.psum_tensor("s_ps", [P, TILES, D], F32))
        t_ps = ctx.enter_context(nc.psum_tensor("t_ps", [P, 2, TOK], F32))

        const_loaded = sem("const_loaded")
        const_set = sem("const_set")
        ident_set = sem("ident_set")
        x_loaded = [sem(f"x_loaded{i}") for i in range(2)]
        adj_loaded = [sem(f"adj_loaded{i}") for i in range(2)]
        adj_eye = sem("adj_eye")
        mask_made = sem("mask_made")
        mask_stored = sem("mask_stored")
        in_normed = sem("in_normed")
        x_ready = sem("x_ready")
        w_loaded = [sem(f"w_loaded{i}") for i in range(2)]
        w_hi_done = sem("w_hi_done")
        w_split = sem("w_split")
        mask_loaded = sem("mask_loaded")
        node_scores = sem("node_scores")
        src_done = sem("src_done")
        dst_hi_done = sem("dst_hi_done")
        dst_done = sem("dst_done")
        x_hi_done = sem("x_hi_done")
        x_split = sem("x_split")
        scores_done = sem("scores_done")
        edges_done = sem("edges_done")
        leaky_done = sem("leaky_done")
        max_done = sem("max_done")
        exp_done = sem("exp_done")
        inv_done = sem("inv_done")
        pt_done = sem("pt_done")
        pt_hi_done = sem("pt_hi_done")
        pt_split = sem("pt_split")
        agg_done = sem("agg_done")
        res1_done = sem("res1_done")
        stats_done = sem("stats_done")
        aggr_done = sem("aggr_done")
        eps_done = sem("eps_done")
        rstd_done = sem("rstd_done")
        norm1_done = sem("norm1_done")
        gamma1_done = sem("gamma1_done")
        h_done = sem("h_done")
        h_bias_done = sem("h_bias_done")
        ht_done = sem("ht_done")
        ht_hi_done = sem("ht_hi_done")
        ht_split = sem("ht_split")
        z_done = sem("z_done")
        g_done = sem("g_done")
        g_hi_done = sem("g_hi_done")
        g_split = sem("g_split")
        y_done = sem("y_done")
        res2_done = sem("res2_done")
        norm2_done = sem("norm2_done")
        gamma2_done = sem("gamma2_done")
        xin_loaded = [sem(f"xin_loaded{i}") for i in range(2)]
        adj2_loaded = [sem(f"adj2_loaded{i}") for i in range(2)]
        wo_loaded = sem("wo_loaded")
        wo_hi_done = sem("wo_hi_done")
        wo_split = sem("wo_split")
        x1_done = sem("x1_done")
        norm3_done = sem("norm3_done")
        mask3_done = sem("mask3_done")
        wh_done = sem("wh_done")
        wh_hi_done = sem("wh_hi_done")
        top8_done = sem("top8_done")
        replaced = sem("replaced")
        next8_done = sem("next8_done")
        kept_done = sem("kept_done")
        neg_part = sem("neg_part")
        pos_part = sem("pos_part")
        elu_exp = sem("elu_exp")
        elu_done = sem("elu_done")
        out_ready = sem("out_ready")
        out_stored = [sem(f"out_stored{i}") for i in range(2)]

        block = ctx.enter_context(nc.Block())

        def wait_alone(eng, semaphore, count):
            eng.wait_ge(semaphore, count)
            eng.nop(nofuse=True)

        CHUNKS = 4
        NORMS_IN = GROUPS

        def norm1_index(u):
            return NORMS_IN + (0 if isinstance(u, int) and u == 0 else 2 * u - 1)

        def norm2_index(t):
            last = isinstance(t, int) and t == UNITS - 1
            return NORMS_IN + 2 * t + (1 if last else 2)

        def norm3_index(d):
            return NORMS_IN + 2 * UNITS + d

        def weight_chunk(hi, k):
            w1_part, w2_part = (w1_hi, w2_hi) if hi else (w1_lo, w2_lo)
            if k < 2:
                return w1_part[:, k, :]
            return w2_part[:, (k - 2) * 4:(k - 1) * 4, :].rearrange("p f d -> p (f d)")

        @block.sync
        def _(sp):
            sp.dma_start(ident[:, :], neg_mask[:, 0:P]).then_inc(const_loaded, DMA)
            sp.dma_start(g_raw[:, 0, 0:P], neg_mask[:, P:2 * P]).then_inc(const_loaded, DMA)
            sp.dma_start(b1_col[:, :], b1).then_inc(const_loaded, DMA)
            sp.dma_start(ab_col[:, :], attn_b.partition_broadcast(P)).then_inc(const_loaded, DMA)
            sp.dma_start(vec[:, :, :, :].rearrange("p l v d -> p (l v d)"),
                         vectors.partition_broadcast(P)).then_inc(const_loaded, DMA)

            def load_group(g, slot):
                sp.dma_start(state[:, bass.ds(g, 1), :, :].rearrange("p g c d -> p (g c) d"),
                             dram_group(x_rows, g)).then_inc(x_loaded[slot], DMA)
                sp.dma_start(h_bias[:, slot, :, :].bitcast(I32),
                             dram_group(adj_rows, g)).then_inc(adj_loaded[slot], DMA)

            def store_mask(g, slot):
                wait_alone(sp, mask_made, g + 1)
                sp.dma_start(mask_dram[bass.ds(g, 1), :, :].rearrange("g p n -> (g p) n"),
                             mask[:, slot, :, :].rearrange("p c n -> p (c n)")
                             ).then_inc(mask_stored, DMA)
                wait_alone(sp, mask_stored, DMA * (g + 1))

            load_group(0, 0)
            load_group(1, 1)
            with sp.Fori(0, GROUPS // 2 - 1) as i:
                for slot in range(2):
                    g = 2 * i + slot
                    store_mask(g, slot)
                    load_group(g + 2, slot)
            for slot in range(2):
                store_mask(GROUPS - 2 + slot, slot)

            def load_mask(u):
                slot = u % 2
                g = u % GROUPS
                if not (isinstance(u, int) and u == 0):
                    wait_alone(sp, mask_loaded, DMA * u)
                if not (isinstance(u, int) and u < 2):
                    wait_alone(sp, scores_done, u - 1)
                sp.dma_start(mask[:, bass.ds(slot, 1), :, :].rearrange("p s c n -> p (s c n)"),
                             mask_dram[bass.ds(g, 1), :, :].rearrange("g p n -> (g p) n")
                             ).then_inc(mask_loaded, DMA)

            def load_weights(l, k):
                if k < 2:
                    src = w1[bass.ds(l, 1), k * P:(k + 1) * P, :].rearrange("l p n -> (l p) n")
                    dst = w_raw[:, k % 2, :]
                else:
                    f0 = (k - 2) * 4
                    src = w2[bass.ds(l, 1), f0 * P:(f0 + 4) * P, :].rearrange(
                        "l (f p) d -> p (l f) d", p=P)
                    dst = w_raw[:, k % 2, :].rearrange("p (f d) -> p f d", f=4)
                if not (isinstance(l, int) and l == 0 and k < 2):
                    wait_alone(sp, w_split, CHUNKS * l + k - 1)
                sp.dma_start(dst, src).then_inc(w_loaded[k % 2], DMA)

            def layer_loads(l, units):
                load_weights(l, 2)
                load_weights(l, 3)
                with sp.Fori(0, units) as g:
                    load_mask(l * GROUPS + g + 3)

            load_mask(0)
            load_mask(1)
            load_weights(0, 0)
            load_weights(0, 1)
            load_mask(2)
            with sp.Fori(0, LAYERS - 1) as l:
                layer_loads(l, GROUPS)
                load_weights(l + 1, 0)
                load_weights(l + 1, 1)
            layer_loads(LAYERS - 1, GROUPS - 3)

            wait_alone(sp, g_split, FB * UNITS)
            sp.dma_start(g_raw[:, 0, :].rearrange("p (k d) -> p k d", k=KB),
                         w_out.rearrange("(k p) d -> p k d", p=P)).then_inc(wo_loaded, DMA)
            wait_alone(sp, x_ready, GROUPS + UNITS)
            sp.dma_start(vec[:, 0, 0:2, :].rearrange("p v d -> p (v d)"),
                         a_out.partition_broadcast(P)).then_inc(wo_loaded, DMA)

            def load_again(d, slot):
                if isinstance(d, int) and d < 2:
                    wait_alone(sp, w_split, CHUNKS * LAYERS)
                    wait_alone(sp, res2_done, 2 * UNITS)
                else:
                    wait_alone(sp, x1_done, d - 1)
                    wait_alone(sp, mask3_done, d - 1)
                sp.dma_start(w_raw[:, slot, :].rearrange("p (c d) -> p c d", c=TILES),
                             dram_group(x_rows, d)).then_inc(xin_loaded[slot], DMA)
                sp.dma_start(h_bias[:, slot, :, :].bitcast(I32),
                             dram_group(adj_rows, d)).then_inc(adj2_loaded[slot], DMA)

            def store_out(d, slot):
                wait_alone(sp, out_ready, d + 1)
                sp.dma_start(dram_group(out_rows, d),
                             state[:, bass.ds(d, 1), :, :].rearrange("p g c d -> p (g c) d")
                             ).then_inc(out_stored[slot], DMA)

            load_again(0, 0)
            load_again(1, 1)
            with sp.Fori(0, GROUPS // 2 - 1) as i:
                for slot in range(2):
                    load_again(2 * i + slot + 2, slot)
                    store_out(2 * i + slot, slot)
            for slot in range(2):
                store_out(GROUPS - 2 + slot, slot)
            for slot in range(2):
                sp.wait_ge(out_stored[slot], DMA * (GROUPS // 2))

        @block.gpsimd
        def _(pool):
            nc.gpsimd.memset(minus_half[:, :], -0.5).then_inc(const_set, 1)
            pool.wait_ge(const_set, 1)

            def root(n):
                wait_alone(pool, aggr_done, n + 1)
                nc.gpsimd.tensor_scalar(var_eps[:, :], mean_var[:, :, 1], EPS, None, ALU.add
                                        ).then_inc(eps_done, 1)
                wait_alone(pool, eps_done, n + 1)
                nc.gpsimd.tensor_tensor(rstd[:, :], var_eps[:, :], minus_half[:, :], ALU.pow
                                        ).then_inc(rstd_done, 1)

            def row(l, name, tiles=TILES):
                return vec[:, bass.ds(l, 1), VEC.index(name), :].to_broadcast([P, tiles, D])

            def unit_state(u):
                return state[:, bass.ds(u % GROUPS, 1), :, :].rearrange("p g c d -> p (g c) d")

            def attend(u):
                wait_alone(pool, x_ready, u + 1)
                if not (isinstance(u, int) and u == 0):
                    wait_alone(pool, agg_done, u)
                nc.gpsimd.tensor_copy(x_hi[:, :, :], unit_state(u)).then_inc(x_hi_done, 1)

            def gather_scale(l, u):
                root(norm1_index(u))
                wait_alone(pool, norm1_done, u + 1)
                nc.gpsimd.tensor_tensor(h[:, :, :], h[:, :, :], row(l, "gamma1"), ALU.mult
                                        ).then_inc(gamma1_done, 1)
                wait_alone(pool, gamma1_done, u + 1)
                nc.gpsimd.tensor_tensor(h[:, :, :], h[:, :, :], row(l, "beta1"), ALU.add
                                        ).then_inc(h_done, 1)

            def gather_bias(l, u):
                wait_alone(pool, h_done, u + 1)
                nc.gpsimd.tensor_tensor(
                    h_bias[:, bass.ds(u % 2, 1), :, :].rearrange("p s c d -> p (s c) d"),
                    h[:, :, :], row(l, "b2"), ALU.add).then_inc(h_bias_done, 1)

            def feed_scale(l, t):
                root(norm2_index(t))
                wait_alone(pool, norm2_done, t + 1)
                nc.gpsimd.tensor_tensor(unit_state(t), unit_state(t), row(l, "gamma2"), ALU.mult
                                        ).then_inc(gamma2_done, 1)
                wait_alone(pool, gamma2_done, t + 1)
                nc.gpsimd.tensor_tensor(unit_state(t), unit_state(t), row(l, "beta2"), ALU.add
                                        ).then_inc(x_ready, 1)

            def step(l, t, l_next=None, l_after=None):
                if l_next is not None:
                    gather_scale(l_next, t + 1)
                    gather_bias(l_next, t + 1)
                if l_after is not None:
                    attend(t + 2)
                feed_scale(l, t)

            with pool.Fori(0, GROUPS) as g:
                root(g)
            attend(0)
            gather_scale(0, 0)
            gather_bias(0, 0)
            attend(1)

            with pool.Fori(0, LAYERS - 1) as l:
                with pool.Fori(0, GROUPS) as g:
                    t = l * GROUPS + g
                    step(l, t, (t + 1) // GROUPS, (t + 2) // GROUPS)
            last, t0 = LAYERS - 1, (LAYERS - 1) * GROUPS
            with pool.Fori(0, GROUPS - 2) as g:
                step(last, t0 + g, last, last)
            step(last, UNITS - 2, last)
            step(last, UNITS - 1)

            def add_input(d, slot):
                wait_alone(pool, xin_loaded[slot], DMA * (d // 2 + 1))
                nc.gpsimd.tensor_tensor(unit_state(d), unit_state(d),
                                        w_raw[:, slot, :].rearrange("p (c d) -> p c d", c=TILES),
                                        ALU.add).then_inc(x1_done, 1)
                root(norm3_index(d))

            def add_result(d):
                wait_alone(pool, elu_done, d + 1)
                nc.gpsimd.tensor_tensor(unit_state(d), unit_state(d), prob[:, :, :], ALU.add
                                        ).then_inc(out_ready, 1)

            add_input(0, 0)
            add_input(1, 1)
            with pool.Fori(0, GROUPS // 2 - 1) as i:
                for slot in range(2):
                    add_result(2 * i + slot)
                    add_input(2 * i + slot + 2, slot)
            add_result(GROUPS - 2)
            add_result(GROUPS - 1)

        @block.scalar
        def _(act):
            def unit_state(u):
                return state[:, bass.ds(u % GROUPS, 1), :, :].rearrange("p g c d -> p (g c d)")

            with act.Fori(0, GROUPS) as g:
                act.wait_ge(in_normed, g + 1)
                nc.scalar.activation(unit_state(g), unit_state(g), ACT.Relu).then_inc(x_ready, 1)

            def edge_scores(u):
                act.wait_ge(scores_done, u + 1)
                act.wait_ge(src_done, u + 1)
                for c in range(TILES):
                    ins = nc.scalar.activation(prob[:, c, :], s_ps[:, c, :], ACT.Identity,
                                               bias=src_b[:, c:c + 1])
                ins.then_inc(edges_done, 1)

            def exps(u):
                act.wait_ge(max_done, u + 1)
                for c in range(TILES):
                    ins = nc.scalar.activation(prob[:, c, :], prob[:, c, :], ACT.Exp,
                                               bias=neg_max[:, c:c + 1],
                                               accum_out=row_sum[:, c:c + 1])
                ins.then_inc(exp_done, 1)

            def transposed_hi(u):
                if not (isinstance(u, int) and u == 0):
                    act.wait_ge(agg_done, u)
                act.wait_ge(pt_done, u + 1)
                for b in range(GRAPHS):
                    nc.scalar.activation(pt_hi[:, b, :, :].rearrange("p j i -> p (j i)"),
                                         t_ps[:, b, :], ACT.Copy).then_inc(pt_hi_done, 1)

            def h_hi(v, func=ACT.Copy, base=0):
                if not base:
                    if not (isinstance(v, int) and v == 0):
                        act.wait_ge(z_done, FB * v)
                act.wait_ge(ht_done, v + base + 1)
                for k in range(KB):
                    nc.scalar.activation(ht_hi[:, k, :], t_ps[:, k, :], func).then_inc(ht_hi_done, 1)

            def gelu(l, t, f):
                act.wait_ge(z_done, FB * t + f + 1)
                if f >= 2:
                    act.wait_ge(g_split, FB * t + f - 1)
                nc.scalar.activation(g_raw[:, f % 2, :], z_ps[:, f % 2, :], ACT.Gelu,
                                     bias=b1_col[:, bass.ds(l * FB + f, 1)]).then_inc(g_done, 1)
                act.wait_ge(g_done, FB * t + f + 1)
                nc.scalar.activation(gt_hi[:, f, :], g_raw[:, f % 2, :], ACT.Copy
                                     ).then_inc(g_hi_done, 1)

            def split_weights(l):
                for k in range(CHUNKS):
                    act.wait_ge(w_loaded[k % 2], DMA * (2 * l + k // 2 + 1))
                    nc.scalar.activation(weight_chunk(True, k), w_raw[:, k % 2, :], ACT.Copy
                                         ).then_inc(w_hi_done, 1)

            def step(l, t, gathers=True, attends=True):
                for f in range(FB):
                    gelu(l, t, f)
                if attends:
                    edge_scores(t + 2)
                if gathers:
                    h_hi(t + 1)
                if attends:
                    exps(t + 2)
                    transposed_hi(t + 2)

            edge_scores(0)
            exps(0)
            transposed_hi(0)
            h_hi(0)
            edge_scores(1)
            exps(1)
            transposed_hi(1)
            with act.Fori(0, LAYERS - 1) as l:
                split_weights(l)
                with act.Fori(0, GROUPS) as g:
                    step(l, l * GROUPS + g)
            last, t0 = LAYERS - 1, (LAYERS - 1) * GROUPS
            split_weights(last)
            with act.Fori(0, GROUPS - 2) as g:
                step(last, t0 + g)
            step(last, UNITS - 2, attends=False)
            step(last, UNITS - 1, gathers=False, attends=False)

            act.wait_ge(wo_loaded, 2 * DMA)
            nc.scalar.activation(w1_hi[:, 0, 0:KB * D], g_raw[:, 0, :], ACT.Copy
                                 ).then_inc(wo_hi_done, 1)

            def project_hi(d):
                if not (isinstance(d, int) and d == 0):
                    act.wait_ge(agg_done, UNITS + d)
                for b in range(2):
                    act.wait_ge(wh_done, 2 * d + b + 1)
                    nc.scalar.activation(x_hi[:, 2 * b:2 * b + 2, :], y_ps[:, 2 * b:2 * b + 2, :],
                                         ACT.Copy).then_inc(wh_hi_done, 1)

            def elu(d):
                act.wait_ge(neg_part, d + 1)
                for c in range(TILES):
                    ins = nc.scalar.activation(s_ps[:, c, :], s_ps[:, c, :], ACT.Relu,
                                               scale=row_inv[:, c:c + 1])
                ins.then_inc(pos_part, 1)
                nc.scalar.activation(prob[:, :, :], prob[:, :, :], ACT.Exp).then_inc(elu_exp, 1)

            def relu_hi(d):
                if not (isinstance(d, int) and d == 0):
                    act.wait_ge(wh_done, 2 * d)
                h_hi(d, ACT.Relu, UNITS)

            relu_hi(0)
            project_hi(0)
            with act.Fori(0, GROUPS - 1) as d:
                edge_scores(UNITS + d)
                exps(UNITS + d)
                relu_hi(d + 1)
                transposed_hi(UNITS + d)
                elu(d)
                project_hi(d + 1)
            d = GROUPS - 1
            edge_scores(UNITS + d)
            exps(UNITS + d)
            transposed_hi(UNITS + d)
            elu(d)

        @block.tensor
        def _(pe):
            def split_product(out_ap, pairs):
                for n, (l_hi, l_lo, r_hi, r_lo) in enumerate(pairs):
                    nc.tensor.matmul(out_ap, l_hi, r_hi, start=(n == 0), stop=False)
                    nc.tensor.matmul(out_ap, l_hi, r_lo, start=False, stop=False)
                    ins = nc.tensor.matmul(out_ap, l_lo, r_hi, start=False,
                                           stop=(n == len(pairs) - 1))
                return ins

            def scores(u, slot=None):
                if slot is None:
                    pe.wait_ge(mask_loaded, DMA * (u + 1))
                    slot = u % 2
                pe.wait_ge(dst_done, u + 1)
                for c in range(TILES):
                    first = c // NB * NB
                    nc.tensor.matmul(s_ps[:, c, :], neg_diag[:, :],
                                     mask[:, bass.ds(slot, 1), c, :].rearrange("p s n -> p (s n)"),
                                     start=True, stop=False)
                    for j in range(NB):
                        cols = s_ps[:, c, j * P:(j + 1) * P]
                        for part in (dst_hi, dst_lo):
                            ins = nc.tensor.matmul(
                                cols, part[:, first + j:first + j + 1].to_broadcast([P, P]),
                                ident_r[:, :], start=False,
                                stop=(part is dst_lo and j == NB - 1))
                ins.then_inc(scores_done, 1)

            def transpose_prob(u, ready):
                pe.wait_ge(ready[0], ready[1])
                for b in range(GRAPHS):
                    for j in range(NB):
                        for i in range(NB):
                            at = j * N + i * P
                            ins = nc.tensor.transpose(t_ps[:, b, at:at + P],
                                                      prob[:, b * NB + i, j * P:(j + 1) * P],
                                                      ident[:, :])
                ins.then_inc(pt_done, 1)

            def aggregate(u):
                pe.wait_ge(pt_split, GRAPHS * (u + 1))
                pe.wait_ge(x_split, u + 1)
                for b in range(GRAPHS):
                    for i in range(NB):
                        at = slice(i * P, (i + 1) * P)
                        ins = split_product(s_ps[:, b * NB + i, :],
                                            [(pt_hi[:, b, j, at], pt_lo[:, b, j, at],
                                              x_hi[:, b * NB + j, :], x_lo[:, b * NB + j, :])
                                             for j in range(NB)])
                ins.then_inc(agg_done, 1)

            def transpose_h(ready):
                pe.wait_ge(ready[0], ready[1])
                for k in range(KB):
                    for c in range(TILES):
                        ins = nc.tensor.transpose(t_ps[:, k, c * P:(c + 1) * P],
                                                  h[:, c, k * P:(k + 1) * P], ident[:, :])
                ins.then_inc(ht_done, 1)

            def expand(t, f):
                if f == 0:
                    pe.wait_ge(ht_split, KB * (t + 1))
                if f >= 2:
                    pe.wait_ge(g_done, FB * t + f - 1)
                at = slice(f * P, (f + 1) * P)
                split_product(z_ps[:, f % 2, :],
                              [(w1_hi[:, k, at], w1_lo[:, k, at], ht_hi[:, k, :], ht_lo[:, k, :])
                               for k in range(KB)]).then_inc(z_done, 1)

            def contract(t, c):
                pe.wait_ge(g_split, FB * (t + 1))
                at = slice(c * P, (c + 1) * P)
                ins = split_product(y_ps[:, c, :],
                                    [(gt_hi[:, f, at], gt_lo[:, f, at], w2_hi[:, f, :], w2_lo[:, f, :])
                                     for f in range(FB)])
                if c % 2:
                    ins.then_inc(y_done, 1)

            def step(l, t, gathers=True, attends=True, first=False):
                for f in range(FB):
                    if f == 2 and gathers:
                        aggregate(t + 1)
                    expand(t, f)
                if attends:
                    pe.wait_ge(res1_done, t + 2)
                    scores(t + 2)
                contract(t, 0)
                contract(t, 1)
                if gathers:
                    pe.wait_ge(pt_split, GRAPHS * (t + 2))
                    transpose_h((h_done, t + 2))
                contract(t, 2)
                contract(t, 3)
                if attends:
                    pe.wait_ge(ht_split, KB * (t + 2))
                    transpose_prob(t + 2, (exp_done, t + 3))

            pe.wait_ge(ident_set, 3)
            scores(0)
            transpose_prob(0, (exp_done, 1))
            aggregate(0)
            pe.wait_ge(pt_split, GRAPHS)
            transpose_h((h_done, 1))
            pe.wait_ge(res1_done, 1)
            scores(1)
            pe.wait_ge(ht_split, KB)
            transpose_prob(1, (exp_done, 2))
            with pe.Fori(0, LAYERS - 1) as l:
                wait_alone(pe, w_split, CHUNKS * (l + 1))
                with pe.Fori(0, GROUPS) as g:
                    step(l, l * GROUPS + g)
            last, t0 = LAYERS - 1, (LAYERS - 1) * GROUPS
            pe.wait_ge(w_split, CHUNKS * LAYERS)
            with pe.Fori(0, GROUPS - 2) as g:
                step(last, t0 + g)
            step(last, UNITS - 2, attends=False)
            step(last, UNITS - 1, gathers=False, attends=False)

            def project(d):
                pe.wait_ge(ht_split, KB * (UNITS + d + 1))
                if not (isinstance(d, int) and d == 0):
                    pe.wait_ge(dst_done, UNITS + d)
                    pe.wait_ge(x_split, UNITS + d)
                for c in range(TILES):
                    at = slice(c * P, (c + 1) * P)
                    ins = split_product(y_ps[:, c, :],
                                        [(ht_hi[:, k, at], ht_lo[:, k, at],
                                          w1_hi[:, 0, k * D:(k + 1) * D],
                                          w1_lo[:, 0, k * D:(k + 1) * D]) for k in range(KB)])
                    if c % 2:
                        ins.then_inc(wh_done, 1)

            def final_scores(d):
                if not (isinstance(d, int) and d == 0):
                    pe.wait_ge(elu_done, d)
                pe.wait_ge(mask3_done, d + 1)
                scores(UNITS + d, d % 2)

            pe.wait_ge(wo_split, 1)
            transpose_h((norm3_done, 1))
            project(0)
            with pe.Fori(0, GROUPS - 1) as d:
                final_scores(d)
                pe.wait_ge(pt_split, GRAPHS * (UNITS + d))
                transpose_h((norm3_done, d + 2))
                project(d + 1)
                pe.wait_ge(ht_split, KB * (UNITS + d + 2))
                transpose_prob(UNITS + d, (kept_done, d + 1))
                aggregate(UNITS + d)
            d = GROUPS - 1
            final_scores(d)
            transpose_prob(UNITS + d, (kept_done, d + 1))
            aggregate(UNITS + d)

        @block.vector
        def _(dve):
            def unit_state(u):
                return state[:, bass.ds(u % GROUPS, 1), :, :].rearrange("p g c d -> p (g c) d")

            def tile_state(u, c):
                return state[:, bass.ds(u % GROUPS, 1), c, :].rearrange("p g d -> p (g d)")

            def moments(n, rows):
                for c in range(TILES):
                    ins = nc.vector.bn_stats(stats[:, c, :], rows(c))
                ins.then_inc(stats_done, 1)
                wait_alone(dve, stats_done, n + 1)
                for c in range(TILES):
                    ins = nc.vector.bn_aggr(mean_var[:, c, :], stats[:, c, :])
                ins.then_inc(aggr_done, 1)

            def normalise(n, rows, to, done):
                dve.wait_ge(rstd_done, n + 1)
                for c in range(TILES):
                    ins = nc.vector.tensor_scalar(to(c), rows(c), mean_var[:, c, 0:1],
                                                  rstd[:, c:c + 1], ALU.subtract, ALU.mult)
                ins.then_inc(done, 1)

            dve.wait_ge(const_loaded, 5 * DMA)
            nc.vector.tensor_copy(ident_r[:, :], ident[:, :]).then_inc(ident_set, 1)
            nc.vector.tensor_copy(neg_diag[:, :], g_raw[:, 0, 0:P]).then_inc(ident_set, 2)

            def enter(g, slot, k):
                dve.wait_ge(adj_loaded[slot], DMA * (k + 1))
                edges = h_bias[:, slot, :, :].bitcast(I32)
                for i in range(NB):
                    own = edges[:, i:TILES:NB, i * P:(i + 1) * P]
                    ins = nc.vector.tensor_tensor(own, own, ident[:, :].unsqueeze(1).to_broadcast(
                        [P, GRAPHS, P]), ALU.add)
                ins.then_inc(adj_eye, 1)
                wait_alone(dve, x_loaded[slot], DMA * (k + 1))
                for c in range(TILES):
                    ins = nc.vector.bn_stats(stats[:, c, :], tile_state(g, c))
                ins.then_inc(stats_done, 1)
                wait_alone(dve, stats_done, g + 1)
                for c in range(TILES):
                    ins = nc.vector.bn_aggr(mean_var[:, c, :], stats[:, c, :])
                ins.then_inc(aggr_done, 1)
                dve.wait_ge(adj_eye, g + 1)
                nc.vector.tensor_scalar(mask[:, slot, :, :], edges, 0.0, 1.0, ALU.is_gt,
                                        ALU.subtract).then_inc(mask_made, 1)
                normalise(g, lambda c: tile_state(g, c), lambda c: tile_state(g, c), in_normed)

            with dve.Fori(0, GROUPS // 2) as k:
                for slot in range(2):
                    enter(2 * k + slot, slot, k)

            def node_score(u, rows, w_src, w_dst, bias):
                unused = prob[:, :, :].bitcast(BF16).rearrange("p c (s n) -> p c s n", s=2)
                for s, w in enumerate((w_src, w_dst)):
                    for c in range(TILES):
                        ins = nc.vector.scalar_tensor_tensor(
                            unused[:, c, s, :], rows(c), 1.0, w, ALU.mult, ALU.mult,
                            accum_out=src_dst[:, s, c:c + 1])
                ins.then_inc(node_scores, 1)
                dve.wait_ge(node_scores, u + 1)
                nc.vector.tensor_copy(dst_hi[:, :], src_dst[:, 1, :]).then_inc(dst_hi_done, 1)
                if bias is None:
                    nc.vector.tensor_copy(src_b[:, :], src_dst[:, 0, :]).then_inc(src_done, 1)
                else:
                    nc.vector.tensor_scalar(src_b[:, :], src_dst[:, 0, :], bias, None, ALU.add
                                            ).then_inc(src_done, 1)
                dve.wait_ge(dst_hi_done, u + 1)
                nc.vector.tensor_tensor(dst_lo[:, :], src_dst[:, 1, :], dst_hi[:, :].bitcast(F32),
                                        ALU.subtract).then_inc(dst_done, 1)

            def layer_row(l, name):
                return vec[:, bass.ds(l, 1), VEC.index(name), :].rearrange("p l d -> p (l d)")

            def attend_scores(l, u):
                dve.wait_ge(x_ready, u + 1)
                if not (isinstance(u, int) and u == 0):
                    dve.wait_ge(pt_done, u)
                node_score(u, lambda c: tile_state(u, c), layer_row(l, "w_src"),
                           layer_row(l, "w_dst"), ab_col[:, bass.ds(l, 1)])

            def x_low(u):
                dve.wait_ge(x_hi_done, u + 1)
                nc.vector.tensor_tensor(x_lo[:, :, :], unit_state(u), x_hi[:, :, :].bitcast(F32),
                                        ALU.subtract).then_inc(x_split, 1)

            def row_max(u):
                dve.wait_ge(edges_done, u + 1)
                nc.vector.scalar_tensor_tensor(prob[:, :, :], prob[:, :, :], SLOPE, prob[:, :, :],
                                               ALU.mult, ALU.max).then_inc(leaky_done, 1)
                dve.wait_ge(leaky_done, u + 1)
                nc.vector.tensor_reduce(neg_max[:, :], prob[:, :, :], AX.X, ALU.max, negate=True
                                        ).then_inc(max_done, 1)

            def transposed_low(u):
                for b in range(GRAPHS):
                    dve.wait_ge(pt_hi_done, GRAPHS * u + b + 1)
                    nc.vector.tensor_tensor(
                        pt_lo[:, b, :, :].rearrange("p j i -> p (j i)"), t_ps[:, b, :],
                        pt_hi[:, b, :, :].rearrange("p j i -> p (j i)").bitcast(F32),
                        ALU.subtract).then_inc(pt_split, 1)

            def invert(u):
                dve.wait_ge(exp_done, u + 1)
                nc.vector.reciprocal(row_inv[:, :], row_sum[:, :]).then_inc(inv_done, 1)

            def residual1(u):
                dve.wait_ge(agg_done, u + 1)
                dve.wait_ge(inv_done, u + 1)
                if not (isinstance(u, int) and u == 0):
                    dve.wait_ge(h_bias_done, u)
                    dve.wait_ge(ht_done, u)
                for c in range(TILES):
                    ins = nc.vector.scalar_tensor_tensor(h[:, c, :], s_ps[:, c, :],
                                                         row_inv[:, c:c + 1], tile_state(u, c),
                                                         ALU.mult, ALU.add)
                ins.then_inc(res1_done, 1)

            def norm1_moments(u):
                wait_alone(dve, res1_done, u + 1)
                moments(norm1_index(u), lambda c: h[:, c, :])

            def norm1(u):
                normalise(norm1_index(u), lambda c: h[:, c, :], lambda c: h[:, c, :], norm1_done)

            def h_low(v):
                for k in range(KB):
                    dve.wait_ge(ht_hi_done, KB * v + k + 1)
                    nc.vector.tensor_tensor(ht_lo[:, k, :], t_ps[:, k, :],
                                            ht_hi[:, k, :].bitcast(F32), ALU.subtract
                                            ).then_inc(ht_split, 1)

            def feed_low(t, f):
                dve.wait_ge(g_hi_done, FB * t + f + 1)
                nc.vector.tensor_tensor(gt_lo[:, f, :], g_raw[:, f % 2, :],
                                        gt_hi[:, f, :].bitcast(F32), ALU.subtract
                                        ).then_inc(g_split, 1)

            def residual2(t, b):
                dve.wait_ge(y_done, 2 * t + b + 1)
                dve.wait_ge(h_bias_done, t + 1)
                rows = state[:, bass.ds(t % GROUPS, 1), 2 * b:2 * b + 2, :].rearrange(
                    "p g c d -> p (g c) d")
                hb = h_bias[:, bass.ds(t % 2, 1), 2 * b:2 * b + 2, :].rearrange(
                    "p s c d -> p (s c) d")
                nc.vector.tensor_tensor(rows, y_ps[:, 2 * b:2 * b + 2, :], hb, ALU.add
                                        ).then_inc(res2_done, 1)

            def norm2_moments(t):
                wait_alone(dve, res2_done, 2 * (t + 1))
                moments(norm2_index(t), lambda c: tile_state(t, c))

            def norm2(t):
                normalise(norm2_index(t), lambda c: tile_state(t, c), lambda c: tile_state(t, c),
                          norm2_done)

            def split_weights(l):
                for k in range(CHUNKS):
                    dve.wait_ge(w_hi_done, CHUNKS * l + k + 1)
                    nc.vector.tensor_tensor(weight_chunk(False, k), w_raw[:, k % 2, :],
                                            weight_chunk(True, k).bitcast(F32), ALU.subtract
                                            ).then_inc(w_split, 1)

            def step(t, gathers=True, l_after=None):
                for f in range(FB):
                    feed_low(t, f)
                    if gathers:
                        if f == 2:
                            residual1(t + 1)
                        if f == 3:
                            norm1_moments(t + 1)
                        if f == 4:
                            norm1(t + 1)
                    if f == 6 and l_after is not None:
                        attend_scores(l_after, t + 2)
                if l_after is not None:
                    x_low(t + 2)
                    row_max(t + 2)
                residual2(t, 0)
                if gathers:
                    h_low(t + 1)
                if l_after is not None:
                    invert(t + 2)
                residual2(t, 1)
                norm2_moments(t)
                if l_after is not None:
                    transposed_low(t + 2)
                norm2(t)

            def attend(u):
                attend_scores(0, u)
                x_low(u)
                row_max(u)
                invert(u)
                transposed_low(u)

            attend(0)
            residual1(0)
            norm1_moments(0)
            norm1(0)
            h_low(0)
            attend(1)
            with dve.Fori(0, LAYERS - 1) as l:
                split_weights(l)
                with dve.Fori(0, GROUPS) as g:
                    t = l * GROUPS + g
                    step(t, l_after=(t + 2) // GROUPS)
            last, t0 = LAYERS - 1, (LAYERS - 1) * GROUPS
            split_weights(last)
            with dve.Fori(0, GROUPS - 2) as g:
                step(t0 + g, l_after=last)
            step(UNITS - 2)
            step(UNITS - 1, gathers=False)

            dve.wait_ge(wo_hi_done, 1)
            nc.vector.tensor_tensor(w1_lo[:, 0, 0:KB * D], g_raw[:, 0, :],
                                    w1_hi[:, 0, 0:KB * D].bitcast(F32), ALU.subtract
                                    ).then_inc(wo_split, 1)

            def norm3_moments(d):
                wait_alone(dve, x1_done, d + 1)
                moments(norm3_index(d), lambda c: tile_state(d, c))

            def norm3(d):
                dve.wait_ge(ht_done, UNITS + d)
                normalise(norm3_index(d), lambda c: tile_state(d, c), lambda c: h[:, c, :],
                          norm3_done)

            def relu_low(d):
                for k in range(KB):
                    dve.wait_ge(ht_hi_done, KB * (UNITS + d) + k + 1)
                    nc.vector.scalar_tensor_tensor(ht_lo[:, k, :], t_ps[:, k, :], 0.0,
                                                   ht_hi[:, k, :].bitcast(F32), ALU.max,
                                                   ALU.subtract).then_inc(ht_split, 1)

            def project_low(d):
                for b in range(2):
                    dve.wait_ge(wh_hi_done, 2 * d + b + 1)
                    ins = nc.vector.tensor_tensor(
                        x_lo[:, 2 * b:2 * b + 2, :], y_ps[:, 2 * b:2 * b + 2, :],
                        x_hi[:, 2 * b:2 * b + 2, :].bitcast(F32), ALU.subtract)
                ins.then_inc(x_split, 1)

            def final_mask(d, slot, k):
                dve.wait_ge(adj2_loaded[slot], DMA * (k + 1))
                dve.wait_ge(scores_done, UNITS + d - 1)
                nc.vector.tensor_scalar(mask[:, slot, :, :], h_bias[:, slot, :, :].bitcast(I32),
                                        0.0, 1.0, ALU.is_gt, ALU.subtract).then_inc(mask3_done, 1)

            def keep_top(d):
                spare = g_raw[:, :, :].rearrange("p s (c n) -> p (s c) n", n=N)
                for c in range(TILES):
                    ins = nc.vector.max(top8[:, c, :], prob[:, c, :])
                ins.then_inc(top8_done, 1)
                wait_alone(dve, top8_done, d + 1)
                for c in range(TILES):
                    ins = nc.vector.match_replace(spare[:, c, :], top8[:, c, :], prob[:, c, :], -1.0)
                ins.then_inc(replaced, 1)
                wait_alone(dve, replaced, d + 1)
                for c in range(TILES):
                    ins = nc.vector.max(next8[:, c, :], spare[:, c, :])
                ins.then_inc(next8_done, 1)
                dve.wait_ge(next8_done, d + 1)
                kth = TOP - 8 - 1
                for c in range(TILES):
                    ins = nc.vector.scalar_tensor_tensor(prob[:, c, :], prob[:, c, :],
                                                         next8[:, c, kth:kth + 1], prob[:, c, :],
                                                         ALU.is_ge, ALU.mult)
                ins.then_inc(kept_done, 1)

            def negative_part(d):
                dve.wait_ge(agg_done, UNITS + d + 1)
                wait_alone(dve, inv_done, UNITS + d + 1)
                for c in range(TILES):
                    ins = nc.vector.tensor_scalar(prob[:, c, :], s_ps[:, c, :], row_inv[:, c:c + 1],
                                                  0.0, ALU.mult, ALU.min)
                ins.then_inc(neg_part, 1)

            def join_parts(d):
                dve.wait_ge(pos_part, d + 1)
                dve.wait_ge(elu_exp, d + 1)
                for b in range(2):
                    at = slice(2 * b, 2 * b + 2)
                    ins = nc.vector.scalar_tensor_tensor(prob[:, at, :], prob[:, at, :], -1.0,
                                                         s_ps[:, at, :], ALU.add, ALU.add)
                ins.then_inc(elu_done, 1)

            def project_scores(d):
                if not (isinstance(d, int) and d == 0):
                    dve.wait_ge(out_ready, d)
                dve.wait_ge(wh_done, 2 * d + 2)
                node_score(UNITS + d, lambda c: y_ps[:, c, :], vec[:, 0, 0, :], vec[:, 0, 1, :], None)

            dve.wait_ge(wo_loaded, 2 * DMA)
            norm3_moments(0)
            norm3(0)
            relu_low(0)
            project_low(0)
            final_mask(0, 0, 0)
            project_scores(0)

            def final_step(d, slot_next, k_next):
                u = UNITS + d
                row_max(u)
                norm3_moments(d + 1)
                invert(u)
                keep_top(d)
                norm3(d + 1)
                relu_low(d + 1)
                transposed_low(u)
                negative_part(d)
                project_low(d + 1)
                final_mask(d + 1, slot_next, k_next)
                join_parts(d)
                project_scores(d + 1)

            with dve.Fori(0, GROUPS // 2 - 1) as k:
                final_step(2 * k, 1, k)
                final_step(2 * k + 1, 0, k + 1)
            final_step(GROUPS - 2, 1, GROUPS // 2 - 1)
            d = GROUPS - 1
            row_max(UNITS + d)
            invert(UNITS + d)
            keep_top(d)
            transposed_low(UNITS + d)
            negative_part(d)
            join_parts(d)


def kernel(**inputs):
    import numpy as np
    import concourse.bacc as bacc
    from concourse import mybir as mb
    from concourse.bass_utils import run_bass_kernel_spmd

    get = {k: np.ascontiguousarray(v) for k, v in inputs.items()}
    layers, d2 = get["L0_gnn_attn_w"].shape
    d = d2 // 2
    w = get["L0_gnn_attn_w"]
    vectors = np.stack([w[:, :d], w[:, d:], get["L0_gnn_g1"], get["L0_gnn_beta1"], get["L0_gnn_b2"],
                        get["L0_gnn_g2"], get["L0_gnn_beta2"]], axis=1).reshape(-1)
    b1 = get["L0_gnn_b1"]
    b1_cols = b1.reshape(layers, -1, 128).transpose(2, 0, 1).reshape(128, -1)
    eye = np.eye(128, dtype=np.float32)
    arrays = {
        "x": get["x"], "adj": get["adj"], "vectors": vectors, "attn_b": get["L0_gnn_attn_b"],
        "w1": get["L0_gnn_W1"], "b1": b1_cols, "w2": get["L0_gnn_W2"], "w_out": get["L1_gnn_W"],
        "a_out": get["L1_gnn_a"].reshape(-1),
        "diagonals": np.concatenate([eye, eye * np.float32(9e15)], axis=1),
    }
    nc = bacc.Bacc("TRN2", target_bir_lowering=False, num_devices=1)
    arrays = {f"in_{k}": np.ascontiguousarray(v) for k, v in arrays.items()}
    args = [nc.dram_tensor(k, a.shape, mb.dt.from_np(a.dtype), kind="ExternalInput").ap()
            for k, a in arrays.items()]
    out = nc.dram_tensor("out_x", get["x"].shape, mb.dt.float32, kind="ExternalOutput").ap()
    gnn_adjacency_kernel(nc, *args, out)
    r = run_bass_kernel_spmd(nc, [arrays], core_ids=[0])
    return r.results[0]["out_x"]
```

```python
import concourse.bass as bass
from concourse import mybir
from contextlib import ExitStack


def gnn_adjacency_kernel(nc, x, adj, vectors, attn_b, w1, b1, w2, w_out, a_out, neg_mask, out):
    F32 = mybir.dt.float32
    F32R = mybir.dt.float32r
    BF16 = mybir.dt.bfloat16
    I32 = mybir.dt.int32
    ALU = mybir.AluOpType
    ACT = mybir.ActivationFunctionType
    AX = mybir.AxisListType

    P = 128
    BATCH, N, D = x.shape
    LAYERS, HIDDEN = w1.shape[0], w1.shape[2]
    GRAPHS = 2
    GROUPS = BATCH // GRAPHS
    NB = N // P
    KB = D // P
    TILES = GRAPHS * NB
    FB = HIDDEN // P
    TOK = TILES * P
    UNITS = LAYERS * GROUPS
    EPS = 1e-5
    SLOPE = 0.2
    TOP = 16
    DMA = 16
    VEC = ("w_src", "w_dst", "gamma1", "beta1", "b2", "gamma2", "beta2")
    NV = len(VEC)

    x_rows = x.rearrange("b n d -> (b n) d")
    adj_rows = adj.rearrange("b n d -> (b n) d")
    out_rows = out.rearrange("b n d -> (b n) d")

    def dram_group(rows, g):
        return rows[bass.ds(g * TOK, TOK), :].rearrange("(c p) d -> p c d", p=P)

    ctx = ExitStack()
    with ctx:
        def sb(name, shape, dt):
            return ctx.enter_context(nc.sbuf_tensor(name, shape, dt))

        def sem(name):
            return ctx.enter_context(nc.semaphore(name))

        state = sb("state", [P, GROUPS, TILES, D], F32)
        w1_hi = sb("w1_hi", [P, KB, HIDDEN], F32R)
        w1_lo = sb("w1_lo", [P, KB, HIDDEN], F32R)
        w2_hi = sb("w2_hi", [P, FB, D], F32R)
        w2_lo = sb("w2_lo", [P, FB, D], F32R)
        w_raw = sb("w_raw", [P, 2, 1024], F32)
        vec = sb("vec", [P, LAYERS, NV, D], F32)
        mask = sb("mask", [P, 2, TILES, N], BF16)
        prob = sb("prob", [P, TILES, N], F32)
        x_hi = sb("x_hi", [P, TILES, D], F32R)
        x_lo = sb("x_lo", [P, TILES, D], F32R)
        pt_hi = sb("pt_hi", [P, GRAPHS, NB, N], F32R)
        pt_lo = sb("pt_lo", [P, GRAPHS, NB, N], F32R)
        h = sb("h", [P, TILES, D], F32)
        h_bias = sb("h_bias", [P, 2, TILES, D], F32)
        ht_hi = sb("ht_hi", [P, KB, TOK], F32R)
        ht_lo = sb("ht_lo", [P, KB, TOK], F32R)
        g_raw = sb("g_raw", [P, 2, TOK], F32)
        gt_hi = sb("gt_hi", [P, FB, TOK], F32R)
        gt_lo = sb("gt_lo", [P, FB, TOK], F32R)
        ident = sb("ident", [P, P], F32)
        ident_r = sb("ident_r", [P, P], F32R)
        neg_diag = sb("neg_diag", [P, P], BF16)
        b1_col = sb("b1_col", [P, LAYERS * FB], F32)
        ab_col = sb("ab_col", [P, LAYERS], F32)
        src_dst = sb("src_dst", [P, 2, TILES], F32)
        src_b = sb("src_b", [P, TILES], F32)
        dst_hi = sb("dst_hi", [P, TILES], F32R)
        dst_lo = sb("dst_lo", [P, TILES], F32R)
        neg_max = sb("neg_max", [P, TILES], F32)
        row_sum = sb("row_sum", [P, TILES], F32)
        row_inv = sb("row_inv", [P, TILES], F32)
        neg_inv = sb("neg_inv", [P, TILES], F32)
        stats = sb("stats", [P, TILES, 6], F32)
        mean_var = sb("mean_var", [P, TILES, 2], F32)
        var_eps = sb("var_eps", [P, TILES], F32)
        rstd = sb("rstd", [P, TILES], F32)
        minus_half = sb("minus_half", [P, TILES], F32)
        top8 = sb("top8", [P, TILES, 8], F32)
        next8 = sb("next8", [P, TILES, 8], F32)
        table_out = sb("table_out", [P, 2], F32)

        mask_dram = nc.dram_tensor("mask_store", [GROUPS, P, TILES * N], BF16, kind="Internal").ap()

        z_ps = ctx.enter_context(nc.psum_tensor("z_ps", [P, 2, TOK], F32))
        y_ps = ctx.enter_context(nc.psum_tensor("y_ps", [P, TILES, D], F32))
        s_ps = ctx.enter_context(nc.psum_tensor("s_ps", [P, TILES, D], F32))
        t_ps = ctx.enter_context(nc.psum_tensor("t_ps", [P, 2, TOK], F32))

        wh_hi = [gt_hi[:, 2 * i:2 * i + 2, :].rearrange("p f (c d) -> p (f c) d", d=D)
                 for i in range(2)]
        wh_lo = [gt_lo[:, 2 * i:2 * i + 2, :].rearrange("p f (c d) -> p (f c) d", d=D)
                 for i in range(2)]
        elu = [vec[:, 1 + i, 0:TILES, :] for i in range(2)]
        wh_unused = vec[:, 0, 2:2 + TILES, :].bitcast(BF16).rearrange("p c (s n) -> p c s n", s=2)
        agg_ps = z_ps[:, :, :].rearrange("p b (c d) -> p (b c) d", d=D)
        wo_hi, wo_lo = w1_hi[:, 0, :], w1_lo[:, 0, :]

        const_loaded = sem("const_loaded")
        const_set = sem("const_set")
        ident_set = sem("ident_set")
        x_loaded = [sem(f"x_loaded{i}") for i in range(2)]
        adj_loaded = [sem(f"adj_loaded{i}") for i in range(2)]
        adj_eye = sem("adj_eye")
        mask_made = sem("mask_made")
        mask_stored = sem("mask_stored")
        in_normed = sem("in_normed")
        x_ready = sem("x_ready")
        w_loaded = [sem(f"w_loaded{i}") for i in range(2)]
        w_hi_done = sem("w_hi_done")
        w_split = sem("w_split")
        mask_loaded = sem("mask_loaded")
        target_done = sem("target_done")
        source_done = sem("source_done")
        src_done = sem("src_done")
        dst_hi_done = sem("dst_hi_done")
        dst_done = sem("dst_done")
        x_hi_done = sem("x_hi_done")
        x_split = sem("x_split")
        scores_done = sem("scores_done")
        edges_done = sem("edges_done")
        leaky_done = sem("leaky_done")
        max_done = sem("max_done")
        exp_done = sem("exp_done")
        inv_done = sem("inv_done")
        neg_inv_done = sem("neg_inv_done")
        pt_done = sem("pt_done")
        pt_hi_done = sem("pt_hi_done")
        pt_split = sem("pt_split")
        agg_done = sem("agg_done")
        res1_done = sem("res1_done")
        stats_done = sem("stats_done")
        aggr_done = sem("aggr_done")
        eps_done = sem("eps_done")
        rstd_done = sem("rstd_done")
        norm1_done = sem("norm1_done")
        gamma1_done = sem("gamma1_done")
        h_done = sem("h_done")
        h_bias_done = sem("h_bias_done")
        ht_done = sem("ht_done")
        ht_hi_done = sem("ht_hi_done")
        ht_split = sem("ht_split")
        z_done = sem("z_done")
        g_done = sem("g_done")
        g_hi_done = sem("g_hi_done")
        g_split = sem("g_split")
        y_done = sem("y_done")
        res2_done = sem("res2_done")
        norm2_done = sem("norm2_done")
        gamma2_done = sem("gamma2_done")
        xin_loaded = [sem(f"xin_loaded{i}") for i in range(2)]
        adj2_loaded = [sem(f"adj2_loaded{i}") for i in range(2)]
        wo_loaded = sem("wo_loaded")
        wo_hi_done = sem("wo_hi_done")
        wo_split = sem("wo_split")
        x1_done = sem("x1_done")
        norm3_done = sem("norm3_done")
        mask3_done = sem("mask3_done")
        wh_done = sem("wh_done")
        wh_hi_done = sem("wh_hi_done")
        top8_done = sem("top8_done")
        replaced = sem("replaced")
        next8_done = sem("next8_done")
        kept_done = sem("kept_done")
        neg_part = sem("neg_part")
        pos_part = sem("pos_part")
        elu_exp = sem("elu_exp")
        elu_done = sem("elu_done")
        out_ready = sem("out_ready")
        out_stored = [sem(f"out_stored{i}") for i in range(2)]

        block = ctx.enter_context(nc.Block())

        def final_steps(eng, step):
            step(0, 0)
            with eng.Fori(0, GROUPS // 2 - 1) as i:
                step(2 * i + 1, 1)
                step(2 * i + 2, 0)
            step(GROUPS - 1, 1)

        def wait_alone(eng, semaphore, count):
            eng.wait_ge(semaphore, count)
            eng.nop(nofuse=True)

        CHUNKS = 4
        W1_CHUNKS, W2_CHUNKS = (0, 1), (2, 3)
        NORMS_IN = GROUPS

        def norm1_index(u):
            return NORMS_IN + (0 if isinstance(u, int) and u == 0 else 2 * u - 1)

        def norm2_index(t):
            last = isinstance(t, int) and t == UNITS - 1
            return NORMS_IN + 2 * t + (1 if last else 2)

        def norm3_index(d):
            return NORMS_IN + 2 * UNITS + d

        def weight_chunk(hi, k):
            w1_part, w2_part = (w1_hi, w2_hi) if hi else (w1_lo, w2_lo)
            if k < 2:
                return w1_part[:, k, :]
            return w2_part[:, (k - 2) * 4:(k - 1) * 4, :].rearrange("p f d -> p (f d)")

        @block.sync
        def _(sp):
            sp.dma_start(ident[:, :], neg_mask[:, 0:P]).then_inc(const_loaded, DMA)
            sp.dma_start(g_raw[:, 0, 0:P], neg_mask[:, P:2 * P]).then_inc(const_loaded, DMA)
            sp.dma_start(b1_col[:, :], b1).then_inc(const_loaded, DMA)
            sp.dma_start(ab_col[:, :], attn_b.partition_broadcast(P)).then_inc(const_loaded, DMA)
            sp.dma_start(vec[:, :, :, :].rearrange("p l v d -> p (l v d)"),
                         vectors.partition_broadcast(P)).then_inc(const_loaded, DMA)

            def load_group(g, slot):
                sp.dma_start(state[:, bass.ds(g, 1), :, :].rearrange("p g c d -> p (g c) d"),
                             dram_group(x_rows, g)).then_inc(x_loaded[slot], DMA)
                sp.dma_start(h_bias[:, slot, :, :].bitcast(I32),
                             dram_group(adj_rows, g)).then_inc(adj_loaded[slot], DMA)

            def store_mask(g, slot):
                wait_alone(sp, mask_made, g + 1)
                sp.dma_start(mask_dram[bass.ds(g, 1), :, :].rearrange("g p n -> (g p) n"),
                             mask[:, slot, :, :].rearrange("p c n -> p (c n)")
                             ).then_inc(mask_stored, DMA)
                wait_alone(sp, mask_stored, DMA * (g + 1))

            load_group(0, 0)
            load_group(1, 1)
            with sp.Fori(0, GROUPS // 2 - 1) as i:
                for slot in range(2):
                    g = 2 * i + slot
                    store_mask(g, slot)
                    load_group(g + 2, slot)
            for slot in range(2):
                store_mask(GROUPS - 2 + slot, slot)

            def load_mask(u):
                slot = u % 2
                g = u % GROUPS
                if not (isinstance(u, int) and u == 0):
                    wait_alone(sp, mask_loaded, DMA * u)
                if not (isinstance(u, int) and u < 2):
                    wait_alone(sp, scores_done, u - 1)
                sp.dma_start(mask[:, bass.ds(slot, 1), :, :].rearrange("p s c n -> p (s c n)"),
                             mask_dram[bass.ds(g, 1), :, :].rearrange("g p n -> (g p) n")
                             ).then_inc(mask_loaded, DMA)

            def load_weights(l, k):
                if k < 2:
                    src = w1[bass.ds(l, 1), k * P:(k + 1) * P, :].rearrange("l p n -> (l p) n")
                    dst = w_raw[:, k % 2, :]
                else:
                    f0 = (k - 2) * 4
                    src = w2[bass.ds(l, 1), f0 * P:(f0 + 4) * P, :].rearrange(
                        "l (f p) d -> p (l f) d", p=P)
                    dst = w_raw[:, k % 2, :].rearrange("p (f d) -> p f d", f=4)
                if not (isinstance(l, int) and l == 0 and k < 2):
                    wait_alone(sp, w_split, CHUNKS * l + k - 1)
                sp.dma_start(dst, src).then_inc(w_loaded[k % 2], DMA)

            def layer_loads(l, units):
                load_weights(l, 2)
                load_weights(l, 3)
                with sp.Fori(0, units) as g:
                    load_mask(l * GROUPS + g + 3)

            load_mask(0)
            load_mask(1)
            load_weights(0, 0)
            load_weights(0, 1)
            load_mask(2)
            with sp.Fori(0, LAYERS - 1) as l:
                layer_loads(l, GROUPS)
                load_weights(l + 1, 0)
                load_weights(l + 1, 1)
            layer_loads(LAYERS - 1, GROUPS - 3)

            wait_alone(sp, g_split, FB * UNITS)
            sp.dma_start(g_raw[:, 0, :].rearrange("p (k d) -> p k d", k=KB),
                         w_out.rearrange("(k p) d -> p k d", p=P)).then_inc(wo_loaded, DMA)
            wait_alone(sp, x_ready, GROUPS + UNITS)
            sp.dma_start(vec[:, 0, 0:2, :].rearrange("p v d -> p (v d)"),
                         a_out.partition_broadcast(P)).then_inc(wo_loaded, DMA)

            def load_again(d, slot):
                if isinstance(d, int) and d < 2:
                    wait_alone(sp, w_split, CHUNKS * LAYERS)
                    wait_alone(sp, res2_done, 2 * UNITS)
                else:
                    wait_alone(sp, x1_done, d - 1)
                    wait_alone(sp, mask3_done, d - 1)
                sp.dma_start(w_raw[:, slot, :].rearrange("p (c d) -> p c d", c=TILES),
                             dram_group(x_rows, d)).then_inc(xin_loaded[slot], DMA)
                sp.dma_start(h_bias[:, slot, :, :].bitcast(I32),
                             dram_group(adj_rows, d)).then_inc(adj2_loaded[slot], DMA)

            def store_out(d, slot):
                wait_alone(sp, out_ready, d + 1)
                sp.dma_start(dram_group(out_rows, d),
                             state[:, bass.ds(d, 1), :, :].rearrange("p g c d -> p (g c) d")
                             ).then_inc(out_stored[slot], DMA)

            load_again(0, 0)
            load_again(1, 1)
            load_again(2, 0)
            with sp.Fori(0, GROUPS // 2 - 2) as i:
                for slot in range(2):
                    store_out(2 * i + slot, slot)
                    load_again(2 * i + slot + 3, 1 - slot)
            store_out(GROUPS - 4, 0)
            load_again(GROUPS - 1, 1)
            for d in range(GROUPS - 3, GROUPS):
                store_out(d, d % 2)
            for slot in range(2):
                sp.wait_ge(out_stored[slot], DMA * (GROUPS // 2))

        @block.gpsimd
        def _(pool):
            nc.gpsimd.memset(minus_half[:, :], -0.5).then_inc(const_set, 1)
            pool.wait_ge(const_set, 1)

            def root(n):
                wait_alone(pool, aggr_done, n + 1)
                nc.gpsimd.tensor_scalar(var_eps[:, :], mean_var[:, :, 1], EPS, None, ALU.add
                                        ).then_inc(eps_done, 1)
                wait_alone(pool, eps_done, n + 1)
                nc.gpsimd.tensor_tensor(rstd[:, :], var_eps[:, :], minus_half[:, :], ALU.pow
                                        ).then_inc(rstd_done, 1)

            def row(l, name, tiles=TILES):
                return vec[:, bass.ds(l, 1), VEC.index(name), :].to_broadcast([P, tiles, D])

            def unit_state(u):
                return state[:, bass.ds(u % GROUPS, 1), :, :].rearrange("p g c d -> p (g c) d")

            def attend(u):
                wait_alone(pool, x_ready, u + 1)
                if not (isinstance(u, int) and u == 0):
                    wait_alone(pool, agg_done, u)
                nc.gpsimd.tensor_copy(x_hi[:, :, :], unit_state(u)).then_inc(x_hi_done, 1)

            def gather_scale(l, u):
                root(norm1_index(u))
                wait_alone(pool, norm1_done, u + 1)
                nc.gpsimd.tensor_tensor(h[:, :, :], h[:, :, :], row(l, "gamma1"), ALU.mult
                                        ).then_inc(gamma1_done, 1)
                wait_alone(pool, gamma1_done, u + 1)
                nc.gpsimd.tensor_tensor(h[:, :, :], h[:, :, :], row(l, "beta1"), ALU.add
                                        ).then_inc(h_done, 1)

            def gather_bias(l, u):
                wait_alone(pool, h_done, u + 1)
                nc.gpsimd.tensor_tensor(
                    h_bias[:, bass.ds(u % 2, 1), :, :].rearrange("p s c d -> p (s c) d"),
                    h[:, :, :], row(l, "b2"), ALU.add).then_inc(h_bias_done, 1)

            def feed_scale(l, t):
                root(norm2_index(t))
                wait_alone(pool, norm2_done, t + 1)
                nc.gpsimd.tensor_tensor(unit_state(t), unit_state(t), row(l, "gamma2"), ALU.mult
                                        ).then_inc(gamma2_done, 1)
                wait_alone(pool, gamma2_done, t + 1)
                nc.gpsimd.tensor_tensor(unit_state(t), unit_state(t), row(l, "beta2"), ALU.add
                                        ).then_inc(x_ready, 1)

            def step(l, t, l_next=None, l_after=None):
                if l_next is not None:
                    gather_scale(l_next, t + 1)
                if l_after is not None:
                    attend(t + 2)
                if l_next is not None:
                    gather_bias(l_next, t + 1)
                feed_scale(l, t)

            with pool.Fori(0, GROUPS) as g:
                root(g)
            attend(0)
            gather_scale(0, 0)
            gather_bias(0, 0)
            attend(1)

            with pool.Fori(0, LAYERS - 1) as l:
                with pool.Fori(0, GROUPS) as g:
                    t = l * GROUPS + g
                    step(l, t, (t + 1) // GROUPS, (t + 2) // GROUPS)
            last, t0 = LAYERS - 1, (LAYERS - 1) * GROUPS
            with pool.Fori(0, GROUPS - 2) as g:
                step(last, t0 + g, last, last)
            step(last, UNITS - 2, last)
            step(last, UNITS - 1)

            def add_input(d, slot, k):
                wait_alone(pool, xin_loaded[slot], DMA * (k + 1))
                nc.gpsimd.tensor_tensor(unit_state(d), unit_state(d),
                                        w_raw[:, slot, :].rearrange("p (c d) -> p c d", c=TILES),
                                        ALU.add).then_inc(x1_done, 1)

            def final_mask(d, slot, k):
                wait_alone(pool, adj2_loaded[slot], DMA * (k + 1))
                wait_alone(pool, scores_done, UNITS + d - 1)
                nc.gpsimd.tensor_scalar(mask[:, slot, :, :], h_bias[:, slot, :, :].bitcast(I32),
                                        0.0, 1.0, ALU.is_gt, ALU.subtract).then_inc(mask3_done, 1)

            def add_result(d, slot):
                wait_alone(pool, elu_done, d + 1)
                nc.gpsimd.tensor_tensor(unit_state(d), unit_state(d), elu[slot], ALU.add
                                        ).then_inc(out_ready, 1)

            def final_step(k, p):
                last = isinstance(k, int) and k == GROUPS - 1
                if not last:
                    root(norm3_index(k + 1))
                    final_mask(k + 1, 1 - p, (k + 1) // 2)
                if not (isinstance(k, int) and k == 0):
                    add_result(k - 1, 1 - p)
                if not (isinstance(k, int) and k + 2 >= GROUPS):
                    add_input(k + 2, p, (k + 2) // 2)

            add_input(0, 0, 0)
            root(norm3_index(0))
            final_mask(0, 0, 0)
            add_input(1, 1, 0)
            final_step(0, 0)
            with pool.Fori(0, GROUPS // 2 - 2) as i:
                final_step(2 * i + 1, 1)
                final_step(2 * i + 2, 0)
            final_step(GROUPS - 3, 1)
            final_step(GROUPS - 2, 0)
            final_step(GROUPS - 1, 1)
            add_result(GROUPS - 1, 1)

        @block.scalar
        def _(act):
            def unit_state(u):
                return state[:, bass.ds(u % GROUPS, 1), :, :].rearrange("p g c d -> p (g c d)")

            with act.Fori(0, GROUPS) as g:
                act.wait_ge(in_normed, g + 1)
                nc.scalar.activation(unit_state(g), unit_state(g), ACT.Relu).then_inc(x_ready, 1)

            def edge_scores(u):
                act.wait_ge(scores_done, u + 1)
                act.wait_ge(src_done, u + 1)
                if not (isinstance(u, int) and u == 0):
                    act.wait_ge(pt_done, u)
                for c in range(TILES):
                    ins = nc.scalar.activation(prob[:, c, :], s_ps[:, c, :], ACT.Identity,
                                               bias=src_b[:, c:c + 1])
                ins.then_inc(edges_done, 1)

            def exps(u):
                act.wait_ge(max_done, u + 1)
                for c in range(TILES):
                    ins = nc.scalar.activation(prob[:, c, :], prob[:, c, :], ACT.Exp,
                                               bias=neg_max[:, c:c + 1],
                                               accum_out=row_sum[:, c:c + 1])
                ins.then_inc(exp_done, 1)

            def transposed_hi(u):
                if not (isinstance(u, int) and u == 0):
                    act.wait_ge(agg_done, u)
                act.wait_ge(pt_done, u + 1)
                for b in range(GRAPHS):
                    nc.scalar.activation(pt_hi[:, b, :, :].rearrange("p j i -> p (j i)"),
                                         t_ps[:, b, :], ACT.Copy).then_inc(pt_hi_done, 1)

            def h_hi(v, func=ACT.Copy, base=0):
                if not base:
                    if not (isinstance(v, int) and v == 0):
                        act.wait_ge(z_done, FB * v)
                act.wait_ge(ht_done, v + base + 1)
                for k in range(KB):
                    nc.scalar.activation(ht_hi[:, k, :], t_ps[:, k, :], func).then_inc(ht_hi_done, 1)

            def gelu(l, t, f):
                act.wait_ge(z_done, FB * t + f + 1)
                if f >= 2:
                    act.wait_ge(g_split, FB * t + f - 1)
                nc.scalar.activation(g_raw[:, f % 2, :], z_ps[:, f % 2, :], ACT.Gelu,
                                     bias=b1_col[:, bass.ds(l * FB + f, 1)]).then_inc(g_done, 1)
                act.wait_ge(g_done, FB * t + f + 1)
                nc.scalar.activation(gt_hi[:, f, :], g_raw[:, f % 2, :], ACT.Copy
                                     ).then_inc(g_hi_done, 1)

            def split_weights(l, chunks):
                for k in chunks:
                    act.wait_ge(w_loaded[k % 2], DMA * (2 * l + k // 2 + 1))
                    nc.scalar.activation(weight_chunk(True, k), w_raw[:, k % 2, :], ACT.Copy
                                         ).then_inc(w_hi_done, 1)

            def fetch_table(func):
                column = 0 if func is ACT.Exp else 1
                nc.scalar.activation(table_out[:, column:column + 1], ident[:, 0:1], func)

            def step(l, t, gathers=True, attends=True, w1_next=False):
                fetch_table(ACT.Gelu)
                for f in range(FB):
                    if f == 1 and gathers:
                        transposed_hi(t + 1)
                    gelu(l, t, f)
                if w1_next:
                    split_weights(l + 1, W1_CHUNKS)
                if attends:
                    edge_scores(t + 2)
                    fetch_table(ACT.Exp)
                if gathers:
                    h_hi(t + 1)
                if attends:
                    exps(t + 2)

            edge_scores(0)
            exps(0)
            transposed_hi(0)
            split_weights(0, W1_CHUNKS)
            h_hi(0)
            split_weights(0, W2_CHUNKS)
            edge_scores(1)
            exps(1)
            with act.Fori(0, LAYERS - 1) as l:
                with act.Fori(0, GROUPS - 1) as g:
                    step(l, l * GROUPS + g)
                step(l, l * GROUPS + GROUPS - 1, w1_next=True)
                act.wait_ge(y_done, 2 * GROUPS * (l + 1))
                split_weights(l + 1, W2_CHUNKS)
            last, t0 = LAYERS - 1, (LAYERS - 1) * GROUPS
            with act.Fori(0, GROUPS - 2) as g:
                step(last, t0 + g)
            step(last, UNITS - 2, attends=False)
            step(last, UNITS - 1, gathers=False, attends=False)

            act.wait_ge(wo_loaded, 2 * DMA)
            nc.scalar.activation(wo_hi[:, 0:KB * D], g_raw[:, 0, :], ACT.Copy
                                 ).then_inc(wo_hi_done, 1)

            def project_hi(d, p):
                for b in range(2):
                    act.wait_ge(wh_done, 2 * d + b + 1)
                    nc.scalar.activation(wh_hi[p][:, 2 * b:2 * b + 2, :],
                                         y_ps[:, 2 * b:2 * b + 2, :], ACT.Copy
                                         ).then_inc(wh_hi_done, 1)

            def elu_parts(d, p):
                act.wait_ge(agg_done, UNITS + d + 1)
                act.wait_ge(neg_inv_done, d + 1)
                for c in range(TILES):
                    nc.scalar.activation(elu[p][:, c, :], agg_ps[:, c, :], ACT.Relu,
                                         scale=neg_inv[:, c:c + 1]).then_inc(neg_part, 1)
                for c in range(TILES):
                    ins = nc.scalar.activation(agg_ps[:, c, :], agg_ps[:, c, :], ACT.Relu,
                                               scale=row_inv[:, c:c + 1])
                ins.then_inc(pos_part, 1)
                act.wait_ge(neg_part, TILES * (d + 1))
                nc.scalar.activation(elu[p], elu[p], ACT.Exp, scale=-1.0).then_inc(elu_exp, 1)

            def final_step(k, p):
                more = not (isinstance(k, int) and k == GROUPS - 1)
                exps(UNITS + k)
                if more:
                    h_hi(k + 1, ACT.Relu, UNITS)
                if not (isinstance(k, int) and k == 0):
                    elu_parts(k - 1, 1 - p)
                if more:
                    project_hi(k + 1, 1 - p)
                transposed_hi(UNITS + k)
                if more:
                    edge_scores(UNITS + k + 1)

            h_hi(0, ACT.Relu, UNITS)
            project_hi(0, 0)
            edge_scores(UNITS)
            final_steps(act, final_step)
            act.wait_ge(out_ready, GROUPS - 2)
            elu_parts(GROUPS - 1, 1)

        @block.tensor
        def _(pe):
            def split_product(out_ap, pairs, first=True, last=True):
                for n, (l_hi, l_lo, r_hi, r_lo) in enumerate(pairs):
                    nc.tensor.matmul(out_ap, l_hi, r_hi, start=(first and n == 0), stop=False)
                    nc.tensor.matmul(out_ap, l_hi, r_lo, start=False, stop=False)
                    ins = nc.tensor.matmul(out_ap, l_lo, r_hi, start=False,
                                           stop=(last and n == len(pairs) - 1))
                return ins

            def scores(u, slot=None):
                if slot is None:
                    pe.wait_ge(mask_loaded, DMA * (u + 1))
                    slot = u % 2
                pe.wait_ge(dst_done, u + 1)
                for c in range(TILES):
                    first = c // NB * NB
                    nc.tensor.matmul(s_ps[:, c, :], neg_diag[:, :],
                                     mask[:, bass.ds(slot, 1), c, :].rearrange("p s n -> p (s n)"),
                                     start=True, stop=False)
                    for j in range(NB):
                        cols = s_ps[:, c, j * P:(j + 1) * P]
                        for part in (dst_hi, dst_lo):
                            ins = nc.tensor.matmul(
                                cols, part[:, first + j:first + j + 1].to_broadcast([P, P]),
                                ident_r[:, :], start=False,
                                stop=(part is dst_lo and j == NB - 1))
                ins.then_inc(scores_done, 1)

            def transpose_prob(u, ready):
                pe.wait_ge(ready[0], ready[1])
                for b in range(GRAPHS):
                    for j in range(NB):
                        for i in range(NB):
                            at = j * N + i * P
                            ins = nc.tensor.transpose(t_ps[:, b, at:at + P],
                                                      prob[:, b * NB + i, j * P:(j + 1) * P],
                                                      ident[:, :])
                ins.then_inc(pt_done, 1)

            def aggregate(u, to=s_ps, feat_hi=x_hi, feat_lo=x_lo):
                pe.wait_ge(pt_split, GRAPHS * (u + 1))
                pe.wait_ge(x_split, u + 1)
                for b in range(GRAPHS):
                    for i in range(NB):
                        at = slice(i * P, (i + 1) * P)
                        ins = split_product(to[:, b * NB + i, :],
                                            [(pt_hi[:, b, j, at], pt_lo[:, b, j, at],
                                              feat_hi[:, b * NB + j, :], feat_lo[:, b * NB + j, :])
                                             for j in range(NB)])
                ins.then_inc(agg_done, 1)

            def transpose_h(ready):
                pe.wait_ge(ready[0], ready[1])
                for k in range(KB):
                    for c in range(TILES):
                        ins = nc.tensor.transpose(t_ps[:, k, c * P:(c + 1) * P],
                                                  h[:, c, k * P:(k + 1) * P], ident[:, :])
                ins.then_inc(ht_done, 1)

            def expand(t, f):
                if f == 0:
                    pe.wait_ge(ht_split, KB * (t + 1))
                if f >= 2:
                    pe.wait_ge(g_done, FB * t + f - 1)
                at = slice(f * P, (f + 1) * P)
                split_product(z_ps[:, f % 2, :],
                              [(w1_hi[:, k, at], w1_lo[:, k, at], ht_hi[:, k, :], ht_lo[:, k, :])
                               for k in range(KB)]).then_inc(z_done, 1)

            def contract(t, c):
                at = slice(c * P, (c + 1) * P)
                for f in range(FB):
                    if c == 0:
                        pe.wait_ge(g_split, FB * t + f + 1)
                    pairs = [(gt_hi[:, f, at], gt_lo[:, f, at], w2_hi[:, f, :], w2_lo[:, f, :])]
                    ins = split_product(y_ps[:, c, :], pairs, f == 0, f == FB - 1)
                if c % 2:
                    ins.then_inc(y_done, 1)

            def step(t, gathers=True, attends=True):
                for f in range(FB):
                    if f == 1 and gathers:
                        transpose_prob(t + 1, (exp_done, t + 2))
                    if f == 4 and gathers:
                        aggregate(t + 1)
                    expand(t, f)
                contract(t, 0)
                contract(t, 1)
                if attends:
                    pe.wait_ge(res1_done, t + 2)
                    scores(t + 2)
                contract(t, 2)
                if gathers:
                    transpose_h((h_done, t + 2))
                contract(t, 3)

            pe.wait_ge(ident_set, 3)
            scores(0)
            transpose_prob(0, (exp_done, 1))
            aggregate(0)
            pe.wait_ge(pt_split, GRAPHS)
            transpose_h((h_done, 1))
            pe.wait_ge(res1_done, 1)
            scores(1)
            pe.wait_ge(w_split, CHUNKS)
            with pe.Fori(0, LAYERS - 1) as l:
                with pe.Fori(0, GROUPS) as g:
                    step(l * GROUPS + g)
            t0 = (LAYERS - 1) * GROUPS
            with pe.Fori(0, GROUPS - 2) as g:
                step(t0 + g)
            step(UNITS - 2, attends=False)
            step(UNITS - 1, gathers=False, attends=False)

            def project(d):
                pe.wait_ge(ht_split, KB * (UNITS + d + 1))
                if not (isinstance(d, int) and d == 0):
                    pe.wait_ge(dst_done, UNITS + d)
                    pe.wait_ge(x_split, UNITS + d)
                for c in range(TILES):
                    at = slice(c * P, (c + 1) * P)
                    ins = split_product(y_ps[:, c, :],
                                        [(ht_hi[:, k, at], ht_lo[:, k, at],
                                          wo_hi[:, k * D:(k + 1) * D],
                                          wo_lo[:, k * D:(k + 1) * D]) for k in range(KB)])
                    if c % 2:
                        ins.then_inc(wh_done, 1)

            def final_scores(d, p):
                pe.wait_ge(mask3_done, d + 1)
                scores(UNITS + d, p)

            def final_step(k, p):
                more = not (isinstance(k, int) and k == GROUPS - 1)
                if more:
                    pe.wait_ge(pt_split, GRAPHS * (UNITS + k))
                    transpose_h((norm3_done, k + 2))
                    project(k + 1)
                    pe.wait_ge(ht_split, KB * (UNITS + k + 2))
                transpose_prob(UNITS + k, (kept_done, k + 1))
                if more:
                    final_scores(k + 1, 1 - p)
                aggregate(UNITS + k, agg_ps, wh_hi[p], wh_lo[p])

            pe.wait_ge(wo_split, 1)
            transpose_h((norm3_done, 1))
            project(0)
            final_scores(0, 0)
            final_steps(pe, final_step)

        @block.vector
        def _(dve):
            def unit_state(u):
                return state[:, bass.ds(u % GROUPS, 1), :, :].rearrange("p g c d -> p (g c) d")

            def tile_state(u, c):
                return state[:, bass.ds(u % GROUPS, 1), c, :].rearrange("p g d -> p (g d)")

            def block_stats(rows, c0=0, c1=TILES):
                for c in range(c0, c1):
                    ins = nc.vector.bn_stats(stats[:, c, :], rows(c))
                return ins

            def combine_stats(n):
                wait_alone(dve, stats_done, n + 1)
                for c in range(TILES):
                    ins = nc.vector.bn_aggr(mean_var[:, c, :], stats[:, c, :])
                ins.then_inc(aggr_done, 1)

            def moments(n, rows):
                block_stats(rows).then_inc(stats_done, 1)
                combine_stats(n)

            def normalise(n, rows, to, done):
                dve.wait_ge(rstd_done, n + 1)
                for c in range(TILES):
                    ins = nc.vector.tensor_scalar(to(c), rows(c), mean_var[:, c, 0:1],
                                                  rstd[:, c:c + 1], ALU.subtract, ALU.mult)
                ins.then_inc(done, 1)

            dve.wait_ge(const_loaded, 5 * DMA)
            nc.vector.tensor_copy(ident_r[:, :], ident[:, :]).then_inc(ident_set, 1)
            nc.vector.tensor_copy(neg_diag[:, :], g_raw[:, 0, 0:P]).then_inc(ident_set, 2)

            def enter(g, slot, k):
                dve.wait_ge(adj_loaded[slot], DMA * (k + 1))
                edges = h_bias[:, slot, :, :].bitcast(I32)
                for i in range(NB):
                    own = edges[:, i:TILES:NB, i * P:(i + 1) * P]
                    ins = nc.vector.tensor_tensor(own, own, ident[:, :].unsqueeze(1).to_broadcast(
                        [P, GRAPHS, P]), ALU.add)
                ins.then_inc(adj_eye, 1)
                wait_alone(dve, x_loaded[slot], DMA * (k + 1))
                for c in range(TILES):
                    ins = nc.vector.bn_stats(stats[:, c, :], tile_state(g, c))
                ins.then_inc(stats_done, 1)
                wait_alone(dve, stats_done, g + 1)
                for c in range(TILES):
                    ins = nc.vector.bn_aggr(mean_var[:, c, :], stats[:, c, :])
                ins.then_inc(aggr_done, 1)
                dve.wait_ge(adj_eye, g + 1)
                nc.vector.tensor_scalar(mask[:, slot, :, :], edges, 0.0, 1.0, ALU.is_gt,
                                        ALU.subtract).then_inc(mask_made, 1)
                normalise(g, lambda c: tile_state(g, c), lambda c: tile_state(g, c), in_normed)

            with dve.Fori(0, GROUPS // 2) as k:
                for slot in range(2):
                    enter(2 * k + slot, slot, k)

            prob_unused = prob[:, :, :].bitcast(BF16).rearrange("p c (s n) -> p c s n", s=2)

            def node_products(rows, s, w, unused=prob_unused):
                for c in range(TILES):
                    ins = nc.vector.scalar_tensor_tensor(
                        unused[:, c, s, :], rows(c), 1.0, w, ALU.mult, ALU.mult,
                        accum_out=src_dst[:, s, c:c + 1])
                return ins

            def split_target(u, ins):
                ins.then_inc(target_done, 1)
                dve.wait_ge(target_done, u + 1)
                nc.vector.tensor_copy(dst_hi[:, :], src_dst[:, 1, :]).then_inc(dst_hi_done, 1)
                dve.wait_ge(dst_hi_done, u + 1)
                nc.vector.tensor_tensor(dst_lo[:, :], src_dst[:, 1, :], dst_hi[:, :].bitcast(F32),
                                        ALU.subtract).then_inc(dst_done, 1)

            def keep_source(u, ins, bias):
                ins.then_inc(source_done, 1)
                dve.wait_ge(source_done, u + 1)
                nc.vector.tensor_scalar(src_b[:, :], src_dst[:, 0, :], bias, None, ALU.add
                                        ).then_inc(src_done, 1)

            def layer_row(l, name):
                return vec[:, bass.ds(l, 1), VEC.index(name), :].rearrange("p l d -> p (l d)")

            def target_scores(l, u):
                dve.wait_ge(x_ready, u + 1)
                if not (isinstance(u, int) and u == 0):
                    dve.wait_ge(pt_done, u)
                split_target(u, node_products(lambda c: tile_state(u, c), 1,
                                              layer_row(l, "w_dst")))

            def source_scores(l, u):
                keep_source(u, node_products(lambda c: tile_state(u, c), 0,
                                             layer_row(l, "w_src")), ab_col[:, bass.ds(l, 1)])

            def x_low(u):
                dve.wait_ge(x_hi_done, u + 1)
                nc.vector.tensor_tensor(x_lo[:, :, :], unit_state(u), x_hi[:, :, :].bitcast(F32),
                                        ALU.subtract).then_inc(x_split, 1)

            def row_max(u):
                dve.wait_ge(edges_done, u + 1)
                nc.vector.scalar_tensor_tensor(prob[:, :, :], prob[:, :, :], SLOPE, prob[:, :, :],
                                               ALU.mult, ALU.max).then_inc(leaky_done, 1)
                dve.wait_ge(leaky_done, u + 1)
                nc.vector.tensor_reduce(neg_max[:, :], prob[:, :, :], AX.X, ALU.max, negate=True
                                        ).then_inc(max_done, 1)

            def transposed_low(u):
                for b in range(GRAPHS):
                    dve.wait_ge(pt_hi_done, GRAPHS * u + b + 1)
                    nc.vector.tensor_tensor(
                        pt_lo[:, b, :, :].rearrange("p j i -> p (j i)"), t_ps[:, b, :],
                        pt_hi[:, b, :, :].rearrange("p j i -> p (j i)").bitcast(F32),
                        ALU.subtract).then_inc(pt_split, 1)

            def invert(u):
                dve.wait_ge(exp_done, u + 1)
                nc.vector.reciprocal(row_inv[:, :], row_sum[:, :]).then_inc(inv_done, 1)

            def residual1(u):
                dve.wait_ge(agg_done, u + 1)
                dve.wait_ge(inv_done, u + 1)
                if not (isinstance(u, int) and u == 0):
                    dve.wait_ge(h_bias_done, u)
                    dve.wait_ge(ht_done, u)
                for c in range(TILES):
                    ins = nc.vector.scalar_tensor_tensor(h[:, c, :], s_ps[:, c, :],
                                                         row_inv[:, c:c + 1], tile_state(u, c),
                                                         ALU.mult, ALU.add)
                ins.then_inc(res1_done, 1)

            def norm1_stats(u, c0=0, c1=TILES):
                if c0 == 0:
                    wait_alone(dve, res1_done, u + 1)
                return block_stats(lambda c: h[:, c, :], c0, c1)

            def norm1(u):
                normalise(norm1_index(u), lambda c: h[:, c, :], lambda c: h[:, c, :], norm1_done)

            def h_low(v):
                for k in range(KB):
                    dve.wait_ge(ht_hi_done, KB * v + k + 1)
                    nc.vector.tensor_tensor(ht_lo[:, k, :], t_ps[:, k, :],
                                            ht_hi[:, k, :].bitcast(F32), ALU.subtract
                                            ).then_inc(ht_split, 1)

            def feed_low(t, f):
                dve.wait_ge(g_hi_done, FB * t + f + 1)
                nc.vector.tensor_tensor(gt_lo[:, f, :], g_raw[:, f % 2, :],
                                        gt_hi[:, f, :].bitcast(F32), ALU.subtract
                                        ).then_inc(g_split, 1)

            def residual2(t, b):
                dve.wait_ge(y_done, 2 * t + b + 1)
                dve.wait_ge(h_bias_done, t + 1)
                rows = state[:, bass.ds(t % GROUPS, 1), 2 * b:2 * b + 2, :].rearrange(
                    "p g c d -> p (g c) d")
                hb = h_bias[:, bass.ds(t % 2, 1), 2 * b:2 * b + 2, :].rearrange(
                    "p s c d -> p (s c) d")
                nc.vector.tensor_tensor(rows, y_ps[:, 2 * b:2 * b + 2, :], hb, ALU.add
                                        ).then_inc(res2_done, 1)

            def norm2_moments(t):
                wait_alone(dve, res2_done, 2 * (t + 1))
                moments(norm2_index(t), lambda c: tile_state(t, c))

            def norm2(t):
                normalise(norm2_index(t), lambda c: tile_state(t, c), lambda c: tile_state(t, c),
                          norm2_done)

            def split_weights(l, chunks):
                for k in chunks:
                    dve.wait_ge(w_hi_done, CHUNKS * l + k + 1)
                    nc.vector.tensor_tensor(weight_chunk(False, k), w_raw[:, k % 2, :],
                                            weight_chunk(True, k).bitcast(F32), ALU.subtract
                                            ).then_inc(w_split, 1)

            def begin(t, gathers=True):
                feed_low(t, 0)
                if gathers:
                    transposed_low(t + 1)
                    invert(t + 1)
                feed_low(t, 1)
                feed_low(t, 2)

            def complete(t, gathers=True, l_after=None, l_weights=None):
                feed_low(t, 3)
                if gathers:
                    residual1(t + 1)
                    norm1_stats(t + 1, 0, TILES // 2)
                feed_low(t, 4)
                if gathers:
                    norm1_stats(t + 1, TILES // 2, TILES).then_inc(stats_done, 1)
                feed_low(t, 5)
                if gathers:
                    combine_stats(norm1_index(t + 1))
                feed_low(t, 6)
                feed_low(t, 7)
                if gathers:
                    norm1(t + 1)
                if l_after is not None:
                    target_scores(l_after, t + 2)
                    source_scores(l_after, t + 2)
                if l_weights is not None:
                    split_weights(l_weights, W1_CHUNKS)
                residual2(t, 0)
                if l_after is not None:
                    row_max(t + 2)
                if gathers:
                    h_low(t + 1)
                residual2(t, 1)
                if l_after is not None:
                    x_low(t + 2)
                norm2_moments(t)

            def attend(u):
                target_scores(0, u)
                source_scores(0, u)
                row_max(u)
                x_low(u)

            attend(0)
            transposed_low(0)
            invert(0)
            residual1(0)
            norm1_stats(0).then_inc(stats_done, 1)
            combine_stats(norm1_index(0))
            split_weights(0, W1_CHUNKS)
            norm1(0)
            h_low(0)
            split_weights(0, W2_CHUNKS)
            attend(1)
            begin(0)
            with dve.Fori(0, LAYERS - 1) as l:
                with dve.Fori(0, GROUPS - 1) as g:
                    t = l * GROUPS + g
                    complete(t, l_after=(t + 2) // GROUPS)
                    begin(t + 1)
                    norm2(t)
                t = l * GROUPS + GROUPS - 1
                complete(t, l_after=l + 1, l_weights=l + 1)
                split_weights(l + 1, W2_CHUNKS)
                begin(t + 1)
                norm2(t)
            last, t0 = LAYERS - 1, (LAYERS - 1) * GROUPS
            with dve.Fori(0, GROUPS - 2) as g:
                complete(t0 + g, l_after=last)
                begin(t0 + g + 1)
                norm2(t0 + g)
            complete(UNITS - 2)
            begin(UNITS - 1, gathers=False)
            norm2(UNITS - 2)
            complete(UNITS - 1, gathers=False)
            norm2(UNITS - 1)

            dve.wait_ge(wo_hi_done, 1)
            nc.vector.tensor_tensor(wo_lo[:, 0:KB * D], g_raw[:, 0, :],
                                    wo_hi[:, 0:KB * D].bitcast(F32), ALU.subtract
                                    ).then_inc(wo_split, 1)

            def norm3_moments(d):
                wait_alone(dve, x1_done, d + 1)
                moments(norm3_index(d), lambda c: tile_state(d, c))

            def norm3(d):
                dve.wait_ge(ht_done, UNITS + d)
                normalise(norm3_index(d), lambda c: tile_state(d, c), lambda c: h[:, c, :],
                          norm3_done)

            def relu_low(d):
                for k in range(KB):
                    dve.wait_ge(ht_hi_done, KB * (UNITS + d) + k + 1)
                    nc.vector.scalar_tensor_tensor(ht_lo[:, k, :], t_ps[:, k, :], 0.0,
                                                   ht_hi[:, k, :].bitcast(F32), ALU.max,
                                                   ALU.subtract).then_inc(ht_split, 1)

            def project_low(d, p):
                for b in range(2):
                    dve.wait_ge(wh_hi_done, 2 * d + b + 1)
                    ins = nc.vector.tensor_tensor(
                        wh_lo[p][:, 2 * b:2 * b + 2, :], y_ps[:, 2 * b:2 * b + 2, :],
                        wh_hi[p][:, 2 * b:2 * b + 2, :].bitcast(F32), ALU.subtract)
                ins.then_inc(x_split, 1)

            def top_eight(d):
                wait_alone(dve, exp_done, UNITS + d + 1)
                for c in range(TILES):
                    ins = nc.vector.max(top8[:, c, :], prob[:, c, :])
                ins.then_inc(top8_done, 1)
                wait_alone(dve, top8_done, d + 1)
                for c in range(TILES):
                    ins = nc.vector.match_replace(rest[:, c, :], top8[:, c, :], prob[:, c, :], -1.0)
                ins.then_inc(replaced, 1)

            def keep_top(d):
                wait_alone(dve, replaced, d + 1)
                for c in range(TILES):
                    ins = nc.vector.max(next8[:, c, :], rest[:, c, :])
                ins.then_inc(next8_done, 1)
                dve.wait_ge(next8_done, d + 1)
                kth = TOP - 8 - 1
                for c in range(TILES):
                    ins = nc.vector.scalar_tensor_tensor(prob[:, c, :], prob[:, c, :],
                                                         next8[:, c, kth:kth + 1], prob[:, c, :],
                                                         ALU.is_ge, ALU.mult)
                ins.then_inc(kept_done, 1)

            def join_parts(d, p):
                dve.wait_ge(pos_part, d + 1)
                dve.wait_ge(elu_exp, d + 1)
                for b in range(2):
                    at = slice(2 * b, 2 * b + 2)
                    ins = nc.vector.scalar_tensor_tensor(elu[p][:, at, :], elu[p][:, at, :], -1.0,
                                                         agg_ps[:, at, :], ALU.add, ALU.add)
                ins.then_inc(elu_done, 1)

            def project_scores(d):
                dve.wait_ge(wh_done, 2 * d + 2)
                u = UNITS + d
                split_target(u, node_products(lambda c: y_ps[:, c, :], 1, vec[:, 0, 1, :],
                                              wh_unused))
                keep_source(u, node_products(lambda c: y_ps[:, c, :], 0, vec[:, 0, 0, :],
                                             wh_unused), 0.0)

            rest = g_raw[:, :, :].rearrange("p s (c n) -> p (s c) n", n=N)
            dve.wait_ge(wo_loaded, 2 * DMA)
            norm3_moments(0)
            norm3(0)
            relu_low(0)
            project_low(0, 0)
            project_scores(0)

            def final_step(k, p):
                u = UNITS + k
                more = not (isinstance(k, int) and k == GROUPS - 1)
                if more:
                    norm3_moments(k + 1)
                row_max(u)
                if more:
                    norm3(k + 1)
                top_eight(k)
                if more:
                    relu_low(k + 1)
                if not (isinstance(k, int) and k == 0):
                    join_parts(k - 1, 1 - p)
                invert(u)
                dve.wait_ge(inv_done, u + 1)
                nc.vector.tensor_scalar(neg_inv[:, :], row_inv[:, :], -1.0, None, ALU.mult
                                        ).then_inc(neg_inv_done, 1)
                keep_top(k)
                if more:
                    project_low(k + 1, 1 - p)
                    project_scores(k + 1)
                transposed_low(u)

            final_steps(dve, final_step)
            join_parts(GROUPS - 1, 1)


def kernel(**inputs):
    import numpy as np
    import concourse.bacc as bacc
    from concourse import mybir as mb
    from concourse.bass_utils import run_bass_kernel_spmd

    get = {k: np.ascontiguousarray(v) for k, v in inputs.items()}
    layers, d2 = get["L0_gnn_attn_w"].shape
    d = d2 // 2
    w = get["L0_gnn_attn_w"]
    vectors = np.stack([w[:, :d], w[:, d:], get["L0_gnn_g1"], get["L0_gnn_beta1"], get["L0_gnn_b2"],
                        get["L0_gnn_g2"], get["L0_gnn_beta2"]], axis=1).reshape(-1)
    b1 = get["L0_gnn_b1"]
    b1_cols = b1.reshape(layers, -1, 128).transpose(2, 0, 1).reshape(128, -1)
    eye = np.eye(128, dtype=np.float32)
    arrays = {
        "x": get["x"], "adj": get["adj"], "vectors": vectors, "attn_b": get["L0_gnn_attn_b"],
        "w1": get["L0_gnn_W1"], "b1": b1_cols, "w2": get["L0_gnn_W2"], "w_out": get["L1_gnn_W"],
        "a_out": get["L1_gnn_a"].reshape(-1),
        "diagonals": np.concatenate([eye, eye * np.float32(9e15)], axis=1),
    }
    nc = bacc.Bacc("TRN2", target_bir_lowering=False, num_devices=1)
    arrays = {f"in_{k}": np.ascontiguousarray(v) for k, v in arrays.items()}
    args = [nc.dram_tensor(k, a.shape, mb.dt.from_np(a.dtype), kind="ExternalInput").ap()
            for k, a in arrays.items()]
    out = nc.dram_tensor("out_x", get["x"].shape, mb.dt.float32, kind="ExternalOutput").ap()
    gnn_adjacency_kernel(nc, *args, out)
    r = run_bass_kernel_spmd(nc, [arrays], core_ids=[0])
    return r.results[0]["out_x"]
```

```python
import concourse.bass as bass
from concourse import mybir
from contextlib import ExitStack


def gnn_adjacency_kernel(nc, x, adj, vectors, attn_b, w1, b1, w2, w_out, a_out, diagonals, out):
    F32 = mybir.dt.float32
    F32R = mybir.dt.float32r
    BF16 = mybir.dt.bfloat16
    I32 = mybir.dt.int32
    ALU = mybir.AluOpType
    ACT = mybir.ActivationFunctionType
    AX = mybir.AxisListType

    P = 128
    BATCH, N, D = x.shape
    LAYERS, HIDDEN = w1.shape[0], w1.shape[2]
    GRAPHS = 2
    GROUPS = BATCH // GRAPHS
    NB = N // P
    KB = D // P
    TILES = GRAPHS * NB
    FB = HIDDEN // P
    TOK = TILES * P
    UNITS = LAYERS * GROUPS
    EPS = 1e-5
    SLOPE = 0.2
    TOP = 16
    DMA = 16
    VEC = ("w_src", "w_dst", "gamma1", "beta1", "b2", "gamma2", "beta2")
    NV = len(VEC)

    x_rows = x.rearrange("b n d -> (b n) d")
    adj_rows = adj.rearrange("b n d -> (b n) d")
    out_rows = out.rearrange("b n d -> (b n) d")

    def dram_group(rows, g):
        return rows[bass.ds(g * TOK, TOK), :].rearrange("(c p) d -> p c d", p=P)

    ctx = ExitStack()
    with ctx:
        def sb(name, shape, dt):
            return ctx.enter_context(nc.sbuf_tensor(name, shape, dt))

        def sem(name):
            return ctx.enter_context(nc.semaphore(name))

        state = sb("state", [P, GROUPS, TILES, D], F32)
        w1_hi = sb("w1_hi", [P, KB, HIDDEN], F32R)
        w1_lo = sb("w1_lo", [P, KB, HIDDEN], F32R)
        w2_hi = sb("w2_hi", [P, FB, D], F32R)
        w2_lo = sb("w2_lo", [P, FB, D], F32R)
        w_raw = sb("w_raw", [P, 2, 1024], F32)
        vec = sb("vec", [P, LAYERS, NV, D], F32)
        mask = sb("mask", [P, 2, TILES, N], BF16)
        prob = sb("prob", [P, TILES, N], F32)
        x_hi = sb("x_hi", [P, TILES, D], F32R)
        x_lo = sb("x_lo", [P, TILES, D], F32R)
        pt_hi = sb("pt_hi", [P, GRAPHS, NB, N], F32R)
        pt_lo = sb("pt_lo", [P, GRAPHS, NB, N], F32R)
        h = sb("h", [P, TILES, D], F32)
        h_bias = sb("h_bias", [P, 2, TILES, D], F32)
        ht_hi = sb("ht_hi", [P, KB, TOK], F32R)
        ht_lo = sb("ht_lo", [P, KB, TOK], F32R)
        g_raw = sb("g_raw", [P, 2, TOK], F32)
        gt_hi = sb("gt_hi", [P, FB, TOK], F32R)
        gt_lo = sb("gt_lo", [P, FB, TOK], F32R)
        ident = sb("ident", [P, P], F32)
        ident_r = sb("ident_r", [P, P], F32R)
        neg_diag = sb("neg_diag", [P, P], BF16)
        b1_col = sb("b1_col", [P, LAYERS * FB], F32)
        ab_col = sb("ab_col", [P, LAYERS], F32)
        src_dst = sb("src_dst", [P, 2, TILES], F32)
        src_b = sb("src_b", [P, TILES], F32)
        dst_hi = sb("dst_hi", [P, TILES], F32R)
        dst_lo = sb("dst_lo", [P, TILES], F32R)
        neg_max = sb("neg_max", [P, TILES], F32)
        row_sum = sb("row_sum", [P, TILES], F32)
        row_inv = sb("row_inv", [P, TILES], F32)
        neg_inv = sb("neg_inv", [P, TILES], F32)
        stats = sb("stats", [P, TILES, 6], F32)
        mean_var = sb("mean_var", [P, TILES, 2], F32)
        var_eps = sb("var_eps", [P, TILES], F32)
        rstd = sb("rstd", [P, TILES], F32)
        minus_half = sb("minus_half", [P, TILES], F32)
        neg_mean1 = sb("neg_mean1", [P, TILES], F32)
        shift1 = sb("shift1", [P, TILES], F32)
        relu_stats = sb("relu_stats", [P, TILES, 6], F32)
        relu_mean_var = sb("relu_mean_var", [P, TILES, 2], F32)
        relu_var_eps = sb("relu_var_eps", [P, TILES], F32)
        relu_rstd = sb("relu_rstd", [P, TILES], F32)
        neg_mean = sb("neg_mean", [P, TILES], F32)
        relu_shift = sb("relu_shift", [P, TILES], F32)
        top_lists = sb("top_lists", [P, 2, TILES, 8], F32)
        table_out = sb("table_out", [P, 2], F32)

        mask_dram = nc.dram_tensor("mask_store", [GROUPS, P, TILES * N], BF16, kind="Internal").ap()

        z_ps = ctx.enter_context(nc.psum_tensor("z_ps", [P, 2, TOK], F32))
        y_ps = ctx.enter_context(nc.psum_tensor("y_ps", [P, TILES, D], F32))
        s_ps = ctx.enter_context(nc.psum_tensor("s_ps", [P, TILES, D], F32))
        t_ps = ctx.enter_context(nc.psum_tensor("t_ps", [P, 2, TOK], F32))

        top8, next8 = top_lists[:, 0], top_lists[:, 1]
        neg_ident = top_lists[:, :, :, :].rearrange("p l c e -> p (l c e)").bitcast(BF16)

        wh_hi = [gt_hi[:, 2 * i:2 * i + 2, :].rearrange("p f (c d) -> p (f c) d", d=D)
                 for i in range(2)]
        wh_lo = [gt_lo[:, 2 * i:2 * i + 2, :].rearrange("p f (c d) -> p (f c) d", d=D)
                 for i in range(2)]
        elu_neg = vec[:, 1, 0:TILES, :]
        elu_pos = vec[:, 2, 0:TILES, :]
        agg_ps = z_ps[:, :, :].rearrange("p b (c d) -> p (b c) d", d=D)
        wo_hi, wo_lo = x_hi[:, 0:KB, :], x_lo[:, 0:KB, :]
        wo_raw = w_raw[:, 1, 0:KB * D].rearrange("p (k d) -> p k d", k=KB)
        wa, wa_hi, wa_lo = src_dst[:, 0, :], dst_hi, dst_lo

        const_loaded = sem("const_loaded")
        vec_loaded = sem("vec_loaded")
        const_set = sem("const_set")
        ident_set = sem("ident_set")
        x_loaded = sem("x_loaded")
        adj_loaded = sem("adj_loaded")
        edges_marked = sem("edges_marked")
        mask_made = sem("mask_made")
        mask_stored = sem("mask_stored")
        relu_stats_done = sem("relu_stats_done")
        relu_aggr_done = sem("relu_aggr_done")
        relu_eps_done = sem("relu_eps_done")
        relu_rstd_done = sem("relu_rstd_done")
        relu_shift_done = sem("relu_shift_done")
        relu_done = sem("relu_done")
        x_ready = sem("x_ready")
        w_loaded = [sem(f"w_loaded{i}") for i in range(2)]
        w_hi_done = sem("w_hi_done")
        w_split = sem("w_split")
        mask_loaded = sem("mask_loaded")
        target_done = sem("target_done")
        source_done = sem("source_done")
        src_done = sem("src_done")
        dst_hi_done = sem("dst_hi_done")
        dst_done = sem("dst_done")
        x_hi_done = sem("x_hi_done")
        x_split = sem("x_split")
        scores_done = sem("scores_done")
        edges_done = sem("edges_done")
        leaky_done = sem("leaky_done")
        max_done = sem("max_done")
        exp_done = sem("exp_done")
        inv_done = sem("inv_done")
        neg_inv_done = sem("neg_inv_done")
        pt_done = sem("pt_done")
        pt_hi_done = sem("pt_hi_done")
        pt_split = sem("pt_split")
        agg_done = sem("agg_done")
        res1_done = sem("res1_done")
        stats_done = sem("stats_done")
        aggr_done = sem("aggr_done")
        eps_done = sem("eps_done")
        rstd_done = sem("rstd_done")
        neg_mean1_done = sem("neg_mean1_done")
        shift1_done = sem("shift1_done")
        norm1_done = sem("norm1_done")
        gamma1_done = sem("gamma1_done")
        h_done = sem("h_done")
        h_bias_done = sem("h_bias_done")
        ht_done = sem("ht_done")
        ht_hi_done = sem("ht_hi_done")
        ht_split = sem("ht_split")
        z_done = sem("z_done")
        g_done = sem("g_done")
        g_hi_done = sem("g_hi_done")
        g_split = sem("g_split")
        y_done = sem("y_done")
        res2_done = sem("res2_done")
        norm2_done = sem("norm2_done")
        gamma2_done = sem("gamma2_done")
        xin_loaded = [sem(f"xin_loaded{i}") for i in range(2)]
        adj2_loaded = [sem(f"adj2_loaded{i}") for i in range(2)]
        wo_loaded = sem("wo_loaded")
        wo_hi_done = sem("wo_hi_done")
        wo_split = sem("wo_split")
        wa_done = sem("wa_done")
        wa_hi_done = sem("wa_hi_done")
        wa_split = sem("wa_split")
        x1_done = sem("x1_done")
        mask3_done = sem("mask3_done")
        wh_done = sem("wh_done")
        wh_hi_done = sem("wh_hi_done")
        top8_done = sem("top8_done")
        replaced = sem("replaced")
        next8_done = sem("next8_done")
        kept_done = sem("kept_done")
        neg_part = sem("neg_part")
        elu_exp = sem("elu_exp")
        elu_done = sem("elu_done")
        neg_added = sem("neg_added")
        out_ready = sem("out_ready")
        out_stored = [sem(f"out_stored{i}") for i in range(2)]

        block = ctx.enter_context(nc.Block())

        def final_steps(eng, step):
            step(0, 0)
            step(1, 1)
            with eng.Fori(0, GROUPS // 2 - 3) as i:
                step(2 * i + 2, 0)
                step(2 * i + 3, 1)
            for k in range(GROUPS - 4, GROUPS):
                step(k, k % 2)

        def wait_alone(eng, semaphore, count):
            eng.wait_ge(semaphore, count)
            eng.nop(nofuse=True)

        CHUNKS = 4
        W1_CHUNKS, W2_CHUNKS = (0, 1), (2, 3)
        AHEAD = 3

        def norm1_index(u):
            return 0 if isinstance(u, int) and u == 0 else 2 * u - 1

        def norm2_index(t):
            last = isinstance(t, int) and t == UNITS - 1
            return 2 * t + (1 if last else 2)

        def wait_input(eng, u, layer_0):
            if layer_0:
                wait_alone(eng, relu_done, u + 1)
            else:
                wait_alone(eng, x_ready, u - GROUPS + 1)

        def weight_chunk(hi, k):
            w1_part, w2_part = (w1_hi, w2_hi) if hi else (w1_lo, w2_lo)
            if k < 2:
                return w1_part[:, k, :]
            return w2_part[:, (k - 2) * 4:(k - 1) * 4, :].rearrange("p f d -> p (f d)")

        @block.sync
        def _(sp):
            def load_group(g, adj_to):
                if not (isinstance(g, int) and g == 0):
                    wait_alone(sp, x_loaded, DMA * g)
                    wait_alone(sp, adj_loaded, DMA * g)
                sp.dma_start(state[:, bass.ds(g, 1), :, :].rearrange("p g c d -> p (g c) d"),
                             dram_group(x_rows, g)).then_inc(x_loaded, DMA)
                sp.dma_start(adj_to, dram_group(adj_rows, g)).then_inc(adj_loaded, DMA)

            def adj_in_h_bias(g):
                return h_bias[:, g % 2, :, :].bitcast(I32)

            def adj_in_w_raw(g):
                return w_raw[:, bass.ds(g % 2, 1), :].rearrange("p s (c n) -> p (s c) n", n=N
                                                                ).bitcast(I32)

            def store_mask(g):
                if not (isinstance(g, int) and g == 0):
                    wait_alone(sp, mask_stored, DMA * g)
                wait_alone(sp, mask_made, g + 1)
                sp.dma_start(mask_dram[bass.ds(g, 1), :, :].rearrange("g p n -> (g p) n"),
                             mask[:, bass.ds(g % 2, 1), :, :].rearrange("p s c n -> p (s c n)")
                             ).then_inc(mask_stored, DMA)

            def load_mask(u):
                if not (isinstance(u, int) and u == GROUPS):
                    wait_alone(sp, mask_loaded, DMA * (u - GROUPS))
                wait_alone(sp, scores_done, u - 1)
                sp.dma_start(mask[:, bass.ds(u % 2, 1), :, :].rearrange("p s c n -> p (s c n)"),
                             mask_dram[bass.ds(u % GROUPS, 1), :, :].rearrange("g p n -> (g p) n")
                             ).then_inc(mask_loaded, DMA)

            def load_weights(l, k):
                if k < 2:
                    src = w1[bass.ds(l, 1), k * P:(k + 1) * P, :].rearrange("l p n -> (l p) n")
                    dst = w_raw[:, k % 2, :]
                else:
                    f0 = (k - 2) * 4
                    src = w2[bass.ds(l, 1), f0 * P:(f0 + 4) * P, :].rearrange(
                        "l (f p) d -> p (l f) d", p=P)
                    dst = w_raw[:, k % 2, :].rearrange("p (f d) -> p f d", f=4)
                if not (isinstance(l, int) and l == 0 and k < 2):
                    wait_alone(sp, w_split, CHUNKS * l + k - 1)
                sp.dma_start(dst, src).then_inc(w_loaded[k % 2], DMA)

            def load_vectors(l0, l1):
                at = slice(l0 * NV * D, l1 * NV * D)
                sp.dma_start(vec[:, :, :, :].rearrange("p l v d -> p (l v d)")[:, at],
                             vectors[at].partition_broadcast(P)).then_inc(vec_loaded, DMA)

            sp.dma_start(ident[:, :], diagonals[:, 0:P]).then_inc(const_loaded, DMA)
            sp.dma_start(g_raw[:, 0, 0:P], diagonals[:, P:2 * P]).then_inc(const_loaded, DMA)
            sp.dma_start(b1_col[:, :], b1).then_inc(const_loaded, DMA)
            sp.dma_start(ab_col[:, :], attn_b.partition_broadcast(P)).then_inc(const_loaded, DMA)
            load_group(0, adj_in_h_bias(0))
            load_vectors(0, 1)
            load_group(1, adj_in_h_bias(1))
            load_weights(0, 0)
            load_weights(0, 1)
            sp.wait_ge(mask_made, 1)
            load_group(2, adj_in_h_bias(2))
            store_mask(0)
            store_mask(1)
            load_weights(0, 2)
            load_weights(0, 3)
            load_vectors(1, LAYERS)
            sp.wait_ge(w_split, CHUNKS)
            load_group(3, adj_in_w_raw(3))
            load_group(4, adj_in_w_raw(4))
            store_mask(2)
            with sp.Fori(5, GROUPS) as g:
                wait_alone(sp, mask_made, g - 1)
                load_group(g, adj_in_w_raw(g))
                store_mask(g - 2)
            store_mask(GROUPS - 2)
            store_mask(GROUPS - 1)
            load_weights(1, 0)
            load_weights(1, 1)
            sp.wait_ge(mask_stored, DMA * GROUPS)
            for u in range(GROUPS, GROUPS + 3):
                load_mask(u)

            with sp.Fori(1, LAYERS - 1) as l:
                load_weights(l, 2)
                load_weights(l, 3)
                with sp.Fori(0, GROUPS) as g:
                    load_mask(l * GROUPS + g + 3)
                load_weights(l + 1, 0)
                load_weights(l + 1, 1)
            load_weights(LAYERS - 1, 2)
            load_weights(LAYERS - 1, 3)
            sp.wait_ge(w_split, CHUNKS * LAYERS)
            sp.dma_start(w_raw[:, 0, :].rearrange("p (c d) -> p c d", c=TILES),
                         dram_group(x_rows, 0)).then_inc(xin_loaded[0], DMA)
            sp.dma_start(wo_raw, w_out.rearrange("(k p) d -> p k d", p=P)).then_inc(wo_loaded, DMA)
            sp.wait_ge(x_ready, GROUPS)
            sp.dma_start(vec[:, 0, 0:2, :].rearrange("p v d -> p (v d)"),
                         a_out.partition_broadcast(P)).then_inc(wo_loaded, DMA)
            with sp.Fori(0, GROUPS - 3) as g:
                load_mask((LAYERS - 1) * GROUPS + g + 3)

            def load_x(d, slot):
                sp.dma_start(w_raw[:, slot, :].rearrange("p (c d) -> p c d", c=TILES),
                             dram_group(x_rows, d)).then_inc(xin_loaded[slot], DMA)

            def load_adj(d, slot):
                sp.dma_start(h_bias[:, slot, :, :].bitcast(I32),
                             dram_group(adj_rows, d)).then_inc(adj2_loaded[slot], DMA)

            def store_out(d, slot):
                wait_alone(sp, out_ready, d + 1)
                sp.dma_start(dram_group(out_rows, d),
                             state[:, bass.ds(d, 1), :, :].rearrange("p g c d -> p (g c) d")
                             ).then_inc(out_stored[slot], DMA)

            def final_io(j, p):
                if not (isinstance(j, int) and j + 4 >= GROUPS):
                    wait_alone(sp, x1_done, j + 3)
                    load_x(j + 4, p)
                if not (isinstance(j, int) and j + 3 >= GROUPS):
                    wait_alone(sp, mask3_done, j + 2)
                    load_adj(j + 3, 1 - p)
                if not (isinstance(j, int) and j == 0):
                    store_out(j - 1, 1 - p)

            sp.wait_ge(wa_split, 1)
            load_x(1, 1)
            for slot in range(2):
                sp.wait_ge(res2_done, 2 * (UNITS - 1 + slot))
                load_adj(slot, slot)
            for d in (2, 3):
                sp.wait_ge(x1_done, d - 1)
                load_x(d, d % 2)
            sp.wait_ge(mask3_done, 1)
            load_adj(2, 0)
            final_steps(sp, final_io)
            store_out(GROUPS - 1, 1)
            for slot in range(2):
                sp.wait_ge(out_stored[slot], DMA * (GROUPS // 2))

        @block.gpsimd
        def _(pool):
            nc.gpsimd.memset(minus_half[:, :], -0.5).then_inc(const_set, 1)
            pool.wait_ge(const_set, 1)

            def root(n):
                wait_alone(pool, aggr_done, n + 1)
                nc.gpsimd.tensor_scalar(var_eps[:, :], mean_var[:, :, 1], EPS, None, ALU.add
                                        ).then_inc(eps_done, 1)
                wait_alone(pool, eps_done, n + 1)
                nc.gpsimd.tensor_tensor(rstd[:, :], var_eps[:, :], minus_half[:, :], ALU.pow
                                        ).then_inc(rstd_done, 1)

            def relu_root(n):
                wait_alone(pool, relu_aggr_done, n + 1)
                nc.gpsimd.tensor_scalar(relu_var_eps[:, :], relu_mean_var[:, :, 1], EPS, None,
                                        ALU.add)
                nc.gpsimd.tensor_scalar(neg_mean[:, :], relu_mean_var[:, :, 0], -1.0, None,
                                        ALU.mult).then_inc(relu_eps_done, 1)
                wait_alone(pool, relu_eps_done, n + 1)
                if not (isinstance(n, int) and n == 0):
                    wait_alone(pool, relu_done, n)
                nc.gpsimd.tensor_tensor(relu_rstd[:, :], relu_var_eps[:, :], minus_half[:, :],
                                        ALU.pow).then_inc(relu_rstd_done, 1)
                wait_alone(pool, relu_rstd_done, n + 1)
                nc.gpsimd.tensor_tensor(relu_shift[:, :], neg_mean[:, :], relu_rstd[:, :],
                                        ALU.mult).then_inc(relu_shift_done, 1)

            def row(l, name, tiles=TILES):
                return vec[:, bass.ds(l, 1), VEC.index(name), :].to_broadcast([P, tiles, D])

            def unit_state(u):
                return state[:, bass.ds(u % GROUPS, 1), :, :].rearrange("p g c d -> p (g c) d")

            def attend(u, layer_0=False):
                wait_input(pool, u, layer_0)
                if not (isinstance(u, int) and u == 0):
                    wait_alone(pool, agg_done, u)
                nc.gpsimd.tensor_copy(x_hi[:, :, :], unit_state(u)).then_inc(x_hi_done, 1)

            def gather_scale(l, u):
                root(norm1_index(u))
                nc.gpsimd.tensor_scalar(neg_mean1[:, :], mean_var[:, :, 0], -1.0, None, ALU.mult
                                        ).then_inc(neg_mean1_done, 1)
                wait_alone(pool, neg_mean1_done, u + 1)
                wait_alone(pool, rstd_done, norm1_index(u) + 1)
                nc.gpsimd.tensor_tensor(shift1[:, :], neg_mean1[:, :], rstd[:, :], ALU.mult
                                        ).then_inc(shift1_done, 1)
                wait_alone(pool, norm1_done, u + 1)
                nc.gpsimd.tensor_tensor(h[:, :, :], h[:, :, :], row(l, "gamma1"), ALU.mult
                                        ).then_inc(gamma1_done, 1)
                wait_alone(pool, gamma1_done, u + 1)
                nc.gpsimd.tensor_tensor(h[:, :, :], h[:, :, :], row(l, "beta1"), ALU.add
                                        ).then_inc(h_done, 1)

            def gather_bias(l, u):
                wait_alone(pool, h_done, u + 1)
                nc.gpsimd.tensor_tensor(
                    h_bias[:, bass.ds(u % 2, 1), :, :].rearrange("p s c d -> p (s c) d"),
                    h[:, :, :], row(l, "b2"), ALU.add).then_inc(h_bias_done, 1)

            def feed_scale(l, t):
                root(norm2_index(t))
                wait_alone(pool, norm2_done, t + 1)
                nc.gpsimd.tensor_tensor(unit_state(t), unit_state(t), row(l, "gamma2"), ALU.mult
                                        ).then_inc(gamma2_done, 1)
                wait_alone(pool, gamma2_done, t + 1)
                nc.gpsimd.tensor_tensor(unit_state(t), unit_state(t), row(l, "beta2"), ALU.add
                                        ).then_inc(x_ready, 1)

            def step(l, t, l_next=None, l_after=None, attend_0=False, relu_norm=None):
                if l_next is not None:
                    gather_scale(l_next, t + 1)
                if l_after is not None:
                    attend(t + 2, attend_0)
                if l_next is not None:
                    gather_bias(l_next, t + 1)
                if relu_norm is not None:
                    relu_root(relu_norm)
                feed_scale(l, t)

            relu_root(0)
            attend(0, True)
            relu_root(1)
            relu_root(2)
            attend(1, True)
            pool.wait_ge(vec_loaded, DMA)
            gather_scale(0, 0)
            gather_bias(0, 0)
            pool.wait_ge(vec_loaded, 2 * DMA)

            with pool.Fori(0, GROUPS - AHEAD) as t:
                step(0, t, 0, 0, attend_0=True, relu_norm=t + AHEAD)
            step(0, GROUPS - 3, 0, 0, attend_0=True)
            step(0, GROUPS - 2, 0, 1)
            step(0, GROUPS - 1, 1, 1)
            with pool.Fori(1, LAYERS - 1) as l:
                with pool.Fori(0, GROUPS) as g:
                    t = l * GROUPS + g
                    step(l, t, (t + 1) // GROUPS, (t + 2) // GROUPS)
            last, t0 = LAYERS - 1, (LAYERS - 1) * GROUPS
            with pool.Fori(0, GROUPS - 2) as g:
                step(last, t0 + g, last, last)

            def add_input(d, slot, k):
                wait_alone(pool, xin_loaded[slot], DMA * (k + 1))
                nc.gpsimd.tensor_tensor(unit_state(d), unit_state(d),
                                        w_raw[:, slot, :].rearrange("p (c d) -> p c d", c=TILES),
                                        ALU.add).then_inc(x1_done, 1)

            def final_mask(d, slot, k):
                wait_alone(pool, adj2_loaded[slot], DMA * (k + 1))
                wait_alone(pool, scores_done, UNITS + d - 1)
                nc.gpsimd.tensor_scalar(mask[:, slot, :, :], h_bias[:, slot, :, :].bitcast(I32),
                                        0.0, None, ALU.is_le).then_inc(mask3_done, 1)

            def add_result(d):
                wait_alone(pool, elu_done, d + 1)
                nc.gpsimd.tensor_tensor(unit_state(d), unit_state(d), elu_neg, ALU.add
                                        ).then_inc(neg_added, 1)
                wait_alone(pool, neg_added, d + 1)
                nc.gpsimd.tensor_tensor(unit_state(d), unit_state(d), elu_pos, ALU.add
                                        ).then_inc(out_ready, 1)

            def final_step(k, p):
                if not (isinstance(k, int) and k + 3 >= GROUPS):
                    add_input(k + 3, 1 - p, (k + 3) // 2)
                if not (isinstance(k, int) and k + 2 >= GROUPS):
                    relu_root(GROUPS + k + 2)
                    final_mask(k + 2, p, (k + 2) // 2)
                if not (isinstance(k, int) and k == 0):
                    add_result(k - 1)

            add_input(0, 0, 0)
            step(last, UNITS - 2, last, relu_norm=GROUPS)
            final_mask(0, 0, 0)
            add_input(1, 1, 0)
            relu_root(GROUPS + 1)
            feed_scale(last, UNITS - 1)
            final_mask(1, 1, 0)
            add_input(2, 0, 1)
            final_steps(pool, final_step)
            add_result(GROUPS - 1)

        @block.scalar
        def _(act):
            def relu_norm(n, rows, to):
                act.wait_ge(relu_shift_done, n + 1)
                for c in range(TILES):
                    ins = nc.scalar.activation(to(c), rows(c), ACT.Relu, scale=relu_rstd[:, c:c + 1],
                                               bias=relu_shift[:, c:c + 1])
                ins.then_inc(relu_done, 1)

            def state_row(g, c):
                return state[:, bass.ds(g, 1), c, :].rearrange("p g d -> p (g d)")

            def enter(g):
                relu_norm(g, lambda c: state_row(g, c), lambda c: state_row(g, c))

            def edge_scores(u):
                act.wait_ge(scores_done, u + 1)
                act.wait_ge(src_done, u + 1)
                if not (isinstance(u, int) and u == 0):
                    act.wait_ge(pt_done, u)
                for c in range(TILES):
                    ins = nc.scalar.activation(prob[:, c, :], s_ps[:, c, :], ACT.Identity,
                                               bias=src_b[:, c:c + 1])
                ins.then_inc(edges_done, 1)

            def exps(u):
                act.wait_ge(max_done, u + 1)
                for c in range(TILES):
                    ins = nc.scalar.activation(prob[:, c, :], prob[:, c, :], ACT.Exp,
                                               bias=neg_max[:, c:c + 1],
                                               accum_out=row_sum[:, c:c + 1])
                ins.then_inc(exp_done, 1)

            def transposed_hi(u):
                if not (isinstance(u, int) and u == 0):
                    act.wait_ge(agg_done, u)
                act.wait_ge(pt_done, u + 1)
                for b in range(GRAPHS):
                    nc.scalar.activation(pt_hi[:, b, :, :].rearrange("p j i -> p (j i)"),
                                         t_ps[:, b, :], ACT.Copy).then_inc(pt_hi_done, 1)

            def h_hi(v, base=0):
                if not base:
                    if not (isinstance(v, int) and v == 0):
                        act.wait_ge(z_done, FB * v)
                act.wait_ge(ht_done, v + base + 1)
                for k in range(KB):
                    nc.scalar.activation(ht_hi[:, k, :], t_ps[:, k, :], ACT.Copy
                                         ).then_inc(ht_hi_done, 1)

            def norm1(u):
                act.wait_ge(shift1_done, u + 1)
                for c in range(TILES):
                    ins = nc.scalar.activation(h[:, c, :], h[:, c, :], ACT.Identity,
                                               scale=rstd[:, c:c + 1], bias=shift1[:, c:c + 1])
                ins.then_inc(norm1_done, 1)

            def gelu(l, t, f):
                act.wait_ge(z_done, FB * t + f + 1)
                if f >= 2:
                    act.wait_ge(g_split, FB * t + f - 1)
                nc.scalar.activation(g_raw[:, f % 2, :], z_ps[:, f % 2, :], ACT.Gelu,
                                     bias=b1_col[:, bass.ds(l * FB + f, 1)]).then_inc(g_done, 1)
                act.wait_ge(g_done, FB * t + f + 1)
                nc.scalar.activation(gt_hi[:, f, :], g_raw[:, f % 2, :], ACT.Copy
                                     ).then_inc(g_hi_done, 1)

            def split_weights(l, chunks):
                for k in chunks:
                    act.wait_ge(w_loaded[k % 2], DMA * (2 * l + k // 2 + 1))
                    nc.scalar.activation(weight_chunk(True, k), w_raw[:, k % 2, :], ACT.Copy
                                         ).then_inc(w_hi_done, 1)

            def fetch_table(func):
                column = 0 if func is ACT.Exp else 1
                nc.scalar.activation(table_out[:, column:column + 1], ident[:, 0:1], func)

            def step(l, t, gathers=True, attends=True, w1_next=False, enters=False):
                fetch_table(ACT.Gelu)
                for f in range(FB):
                    if f == 4 and enters:
                        enter(t + 2)
                    if f == 1 and gathers:
                        transposed_hi(t + 1)
                    gelu(l, t, f)
                if gathers:
                    norm1(t + 1)
                if w1_next:
                    split_weights(l + 1, W1_CHUNKS)
                if attends:
                    edge_scores(t + 2)
                    fetch_table(ACT.Exp)
                if gathers:
                    h_hi(t + 1)
                if attends:
                    exps(t + 2)

            enter(0)
            edge_scores(0)
            enter(1)
            exps(0)
            transposed_hi(0)
            split_weights(0, W1_CHUNKS)
            norm1(0)
            edge_scores(1)
            exps(1)
            split_weights(0, W2_CHUNKS)
            h_hi(0)
            def last_step(l):
                step(l, l * GROUPS + GROUPS - 1, w1_next=True)
                act.wait_ge(y_done, 2 * GROUPS * (l + 1))
                split_weights(l + 1, W2_CHUNKS)

            with act.Fori(0, GROUPS - AHEAD) as t:
                step(0, t, enters=True)
            step(0, GROUPS - 3, enters=True)
            step(0, GROUPS - 2)
            last_step(0)
            with act.Fori(1, LAYERS - 1) as l:
                with act.Fori(0, GROUPS - 1) as g:
                    step(l, l * GROUPS + g)
                last_step(l)
            last, t0 = LAYERS - 1, (LAYERS - 1) * GROUPS
            with act.Fori(0, GROUPS - 2) as g:
                step(last, t0 + g)
            step(last, UNITS - 2, attends=False)

            def project_hi(d, p):
                for b in range(2):
                    act.wait_ge(wh_done, 2 * d + b + 1)
                    nc.scalar.activation(wh_hi[p][:, 2 * b:2 * b + 2, :],
                                         y_ps[:, 2 * b:2 * b + 2, :], ACT.Copy
                                         ).then_inc(wh_hi_done, 1)

            def elu_parts(d):
                act.wait_ge(agg_done, UNITS + d + 1)
                act.wait_ge(neg_inv_done, d + 1)
                if not (isinstance(d, int) and d == 0):
                    act.wait_ge(out_ready, d)
                for c in range(TILES):
                    ins = nc.scalar.activation(elu_neg[:, c, :], agg_ps[:, c, :], ACT.Relu,
                                               scale=neg_inv[:, c:c + 1])
                ins.then_inc(neg_part, 1)
                for c in range(TILES):
                    nc.scalar.activation(elu_pos[:, c, :], agg_ps[:, c, :], ACT.Relu,
                                         scale=row_inv[:, c:c + 1])
                act.wait_ge(neg_part, d + 1)
                nc.scalar.activation(elu_neg, elu_neg, ACT.Exp, scale=-1.0).then_inc(elu_exp, 1)
                act.wait_ge(elu_exp, d + 1)
                nc.scalar.activation(elu_neg, elu_neg, ACT.Copy, bias=-1.0).then_inc(elu_done, 1)

            def final_edges(d):
                u = UNITS + d
                act.wait_ge(scores_done, u + 1)
                act.wait_ge(pt_done, u)
                nc.scalar.activation(prob[:, :, :], s_ps[:, :, :], ACT.Copy).then_inc(edges_done, 1)

            def final_norm(d):
                act.wait_ge(ht_done, UNITS + d)
                relu_norm(GROUPS + d, lambda c: state_row(d, c), lambda c: h[:, c, :])

            def final_step(k, p):
                more = not (isinstance(k, int) and k == GROUPS - 1)
                exps(UNITS + k)
                if not (isinstance(k, int) and k == 0):
                    elu_parts(k - 1)
                if more:
                    project_hi(k + 1, 1 - p)
                two_more = not (isinstance(k, int) and k + 2 >= GROUPS)
                if two_more:
                    final_norm(k + 2)
                transposed_hi(UNITS + k)
                if more:
                    final_edges(k + 1)
                if two_more:
                    h_hi(k + 2, UNITS)

            act.wait_ge(wo_loaded, 2 * DMA)
            act.wait_ge(agg_done, UNITS)
            nc.scalar.activation(wo_hi, wo_raw, ACT.Copy).then_inc(wo_hi_done, 1)
            for f in range(FB):
                if f == 4:
                    final_norm(0)
                gelu(last, UNITS - 1, f)
            h_hi(0, UNITS)
            final_norm(1)
            project_hi(0, 0)
            final_edges(0)
            h_hi(1, UNITS)
            final_steps(act, final_step)
            elu_parts(GROUPS - 1)

        @block.tensor
        def _(pe):
            def split_product(out_ap, pairs, first=True, last=True):
                for n, (l_hi, l_lo, r_hi, r_lo) in enumerate(pairs):
                    nc.tensor.matmul(out_ap, l_hi, r_hi, start=(first and n == 0), stop=False)
                    nc.tensor.matmul(out_ap, l_hi, r_lo, start=False, stop=False)
                    ins = nc.tensor.matmul(out_ap, l_lo, r_hi, start=False,
                                           stop=(last and n == len(pairs) - 1))
                return ins

            def scores(u, layer_0=False):
                if layer_0:
                    pe.wait_ge(mask_made, u + 1)
                else:
                    pe.wait_ge(mask_loaded, DMA * (u - GROUPS + 1))
                pe.wait_ge(dst_done, u + 1)
                for b in range(GRAPHS):
                    tiles = slice(b * NB, (b + 1) * NB)
                    nc.tensor.matmul(s_ps[:, tiles, :].rearrange("p c n -> p (c n)"), neg_diag[:, :],
                                     mask[:, bass.ds(u % 2, 1), tiles, :].rearrange(
                                         "p s c n -> p (s c n)"), start=True, stop=False)
                    for j in range(NB):
                        for part in (dst_hi, dst_lo):
                            at = b * NB + j
                            ins = nc.tensor.matmul(
                                s_ps[:, tiles, j * P:(j + 1) * P],
                                part[:, at:at + 1].to_broadcast([P, P]),
                                ident_r[:, :].unsqueeze(1).to_broadcast([P, NB, P]),
                                start=False, stop=(part is dst_lo and j == NB - 1))
                ins.then_inc(scores_done, 1)

            def transpose_prob(u, ready):
                pe.wait_ge(ready[0], ready[1])
                for b in range(GRAPHS):
                    for j in range(NB):
                        for i in range(NB):
                            at = j * N + i * P
                            ins = nc.tensor.transpose(t_ps[:, b, at:at + P],
                                                      prob[:, b * NB + i, j * P:(j + 1) * P],
                                                      ident[:, :])
                ins.then_inc(pt_done, 1)

            def aggregate(u, to=s_ps, feat_hi=x_hi, feat_lo=x_lo):
                pe.wait_ge(pt_split, GRAPHS * (u + 1))
                pe.wait_ge(x_split, u + 1)
                for b in range(GRAPHS):
                    for i in range(NB):
                        at = slice(i * P, (i + 1) * P)
                        ins = split_product(to[:, b * NB + i, :],
                                            [(pt_hi[:, b, j, at], pt_lo[:, b, j, at],
                                              feat_hi[:, b * NB + j, :], feat_lo[:, b * NB + j, :])
                                             for j in range(NB)])
                ins.then_inc(agg_done, 1)

            def transpose_h(ready):
                pe.wait_ge(ready[0], ready[1])
                for k in range(KB):
                    for c in range(TILES):
                        ins = nc.tensor.transpose(t_ps[:, k, c * P:(c + 1) * P],
                                                  h[:, c, k * P:(k + 1) * P], ident[:, :])
                ins.then_inc(ht_done, 1)

            def expand(t, f):
                if f == 0:
                    pe.wait_ge(ht_split, KB * (t + 1))
                if f >= 2:
                    pe.wait_ge(g_done, FB * t + f - 1)
                at = slice(f * P, (f + 1) * P)
                split_product(z_ps[:, f % 2, :],
                              [(w1_hi[:, k, at], w1_lo[:, k, at], ht_hi[:, k, :], ht_lo[:, k, :])
                               for k in range(KB)]).then_inc(z_done, 1)

            def contract(t, c):
                at = slice(c * P, (c + 1) * P)
                for f in range(FB):
                    if c == 0:
                        pe.wait_ge(g_split, FB * t + f + 1)
                    pairs = [(gt_hi[:, f, at], gt_lo[:, f, at], w2_hi[:, f, :], w2_lo[:, f, :])]
                    ins = split_product(y_ps[:, c, :], pairs, f == 0, f == FB - 1)
                if c % 2:
                    ins.then_inc(y_done, 1)

            def step(t, gathers=True, attends=True, attend_0=False):
                for f in range(FB):
                    if f == 1 and gathers:
                        transpose_prob(t + 1, (exp_done, t + 2))
                    if f == 4 and gathers:
                        aggregate(t + 1)
                    expand(t, f)
                contract(t, 0)
                contract(t, 1)
                if attends:
                    pe.wait_ge(res1_done, t + 2)
                    scores(t + 2, layer_0=attend_0)
                contract(t, 2)
                if gathers:
                    transpose_h((h_done, t + 2))
                contract(t, 3)

            pe.wait_ge(ident_set, 4)
            scores(0, layer_0=True)
            transpose_prob(0, (exp_done, 1))
            aggregate(0)
            pe.wait_ge(res1_done, 1)
            scores(1, layer_0=True)
            transpose_h((h_done, 1))
            pe.wait_ge(w_split, CHUNKS)
            with pe.Fori(0, GROUPS - AHEAD) as t:
                step(t, attend_0=True)
            step(GROUPS - 3, attend_0=True)
            step(GROUPS - 2)
            step(GROUPS - 1)
            with pe.Fori(1, LAYERS - 1) as l:
                with pe.Fori(0, GROUPS) as g:
                    step(l * GROUPS + g)
            t0 = (LAYERS - 1) * GROUPS
            with pe.Fori(0, GROUPS - 2) as g:
                step(t0 + g)
            step(UNITS - 2, attends=False)

            def project(d):
                pe.wait_ge(ht_split, KB * (UNITS + d + 1))
                if isinstance(d, int) and d == 0:
                    pe.wait_ge(res2_done, 2 * UNITS)
                else:
                    pe.wait_ge(x_split, UNITS + d)
                for c in range(TILES):
                    at = slice(c * P, (c + 1) * P)
                    ins = split_product(y_ps[:, c, :],
                                        [(ht_hi[:, k, at], ht_lo[:, k, at],
                                          wo_hi[:, k, :], wo_lo[:, k, :]) for k in range(KB)])
                    if c % 2:
                        ins.then_inc(wh_done, 1)

            def source_part(c, last):
                own = slice(c * P, (c + 1) * P)
                return split_product(s_ps[:, c, :],
                                     [(ht_hi[:, k, own], ht_lo[:, k, own],
                                       wa_hi[:, k:k + 1].to_broadcast([P, N]),
                                       wa_lo[:, k:k + 1].to_broadcast([P, N]))
                                      for k in range(KB)], first=False, last=last)

            def final_scores(d, p):
                pe.wait_ge(mask3_done, d + 1)
                if not (isinstance(d, int) and d == 0):
                    pe.wait_ge(edges_done, UNITS + d)
                for b in range(GRAPHS):
                    tiles = slice(b * NB, (b + 1) * NB)
                    nc.tensor.matmul(s_ps[:, tiles, :].rearrange("p c n -> p (c n)"), neg_diag[:, :],
                                     mask[:, p, tiles, :].rearrange("p c n -> p (c n)"),
                                     start=True, stop=False)
                    hts = [part[:, :, b * N:(b + 1) * N] for part in (ht_hi, ht_lo)]
                    split_product(s_ps[:, tiles, :],
                                  [(wa_hi[:, KB + k:KB + k + 1].to_broadcast([P, P]),
                                    wa_lo[:, KB + k:KB + k + 1].to_broadcast([P, P]),
                                    *(part[:, k, :].unsqueeze(1).to_broadcast([P, NB, N])
                                      for part in hts)) for k in range(KB)],
                                  first=False, last=False)
                    for c in range(b * NB, (b + 1) * NB):
                        if c < TILES - 1:
                            source_part(c, c % NB == NB - 1)

            def final_scores_end():
                source_part(TILES - 1, True).then_inc(scores_done, 1)

            def final_step(k, p):
                more = not (isinstance(k, int) and k == GROUPS - 1)
                if more:
                    project(k + 1)
                    final_scores(k + 1, 1 - p)
                transpose_prob(UNITS + k, (kept_done, k + 1))
                if more:
                    final_scores_end()
                if not (isinstance(k, int) and k + 2 >= GROUPS):
                    pe.wait_ge(pt_split, GRAPHS * (UNITS + k + 1))
                    transpose_h((relu_done, GROUPS + k + 3))
                if not (isinstance(k, int) and k == 0):
                    pe.wait_ge(elu_done, k)
                aggregate(UNITS + k, agg_ps, wh_hi[p], wh_lo[p])

            for f in range(FB):
                expand(UNITS - 1, f)
            transpose_h((relu_done, GROUPS + 1))
            for c in range(TILES):
                contract(UNITS - 1, c)
            pe.wait_ge(wa_split, 1)
            pe.wait_ge(ht_split, KB * (UNITS + 1))
            final_scores(0, 0)
            final_scores_end()
            project(0)
            transpose_h((relu_done, GROUPS + 2))
            final_steps(pe, final_step)

        @block.vector
        def _(dve):
            def unit_state(u):
                return state[:, bass.ds(u % GROUPS, 1), :, :].rearrange("p g c d -> p (g c) d")

            def tile_state(u, c):
                return state[:, bass.ds(u % GROUPS, 1), c, :].rearrange("p g d -> p (g d)")

            def block_stats(rows, c0=0, c1=TILES):
                for c in range(c0, c1):
                    ins = nc.vector.bn_stats(stats[:, c, :], rows(c))
                return ins

            def combine_stats(n):
                wait_alone(dve, stats_done, n + 1)
                for c in range(TILES):
                    ins = nc.vector.bn_aggr(mean_var[:, c, :], stats[:, c, :])
                ins.then_inc(aggr_done, 1)

            def moments(n, rows):
                block_stats(rows).then_inc(stats_done, 1)
                combine_stats(n)

            def normalise(n, rows, to, done):
                dve.wait_ge(rstd_done, n + 1)
                for c in range(TILES):
                    ins = nc.vector.tensor_scalar(to(c), rows(c), mean_var[:, c, 0:1],
                                                  rstd[:, c:c + 1], ALU.subtract, ALU.mult)
                ins.then_inc(done, 1)

            dve.wait_ge(const_loaded, 4 * DMA)
            nc.vector.tensor_copy(ident_r[:, :], ident[:, :]).then_inc(ident_set, 1)
            nc.vector.tensor_copy(neg_diag[:, :], g_raw[:, 0, 0:P]).then_inc(ident_set, 1)
            nc.vector.tensor_scalar(neg_ident, ident[:, :], -1.0, None, ALU.mult
                                    ).then_inc(ident_set, 2)

            def relu_moments(n, rows):
                if not (isinstance(n, int) and n == 0):
                    wait_alone(dve, relu_shift_done, n)
                for c in range(TILES):
                    ins = nc.vector.bn_stats(relu_stats[:, c, :], rows(c))
                ins.then_inc(relu_stats_done, 1)
                wait_alone(dve, relu_stats_done, n + 1)
                for c in range(TILES):
                    ins = nc.vector.bn_aggr(relu_mean_var[:, c, :], relu_stats[:, c, :])
                ins.then_inc(relu_aggr_done, 1)

            def enter(g):
                wait_alone(dve, x_loaded, DMA * (g + 1))
                relu_moments(g, lambda c: tile_state(g, c))

            def enter_mask(g, adjacency):
                dve.wait_ge(adj_loaded, DMA * (g + 1))
                if not (isinstance(g, int) and g < 2):
                    dve.wait_ge(scores_done, g - 1)
                    dve.wait_ge(mask_stored, DMA * (g - 1))
                at = bass.ds(g % 2, 1)
                nc.vector.tensor_scalar(
                    mask[:, at, :, :].rearrange("p s c n -> p (s c) n"), adjacency,
                    0.0, None, ALU.is_le).then_inc(edges_marked, 1)
                dve.wait_ge(edges_marked, g + 1)
                for i in range(NB):
                    own = mask[:, at, i:TILES:NB, i * P:(i + 1) * P].rearrange(
                        "p s c n -> p (s c) n")
                    ins = nc.vector.tensor_tensor(
                        own, adjacency[:, i:TILES:NB, i * P:(i + 1) * P],
                        neg_ident.unsqueeze(1).to_broadcast([P, GRAPHS, P]), ALU.is_le)
                ins.then_inc(mask_made, 1)

            def adj_in_h_bias(g):
                return h_bias[:, g % 2, :, :].bitcast(I32)

            def adj_in_w_raw(g):
                return w_raw[:, bass.ds(g % 2, 1), :].rearrange("p s (c n) -> p (s c) n", n=N
                                                                ).bitcast(I32)

            prob_unused = prob[:, :, :].bitcast(BF16).rearrange("p c (s n) -> p c s n", s=2)

            def node_products(rows, s, w):
                for c in range(TILES):
                    ins = nc.vector.scalar_tensor_tensor(
                        prob_unused[:, c, s, :], rows(c), 1.0, w, ALU.mult, ALU.mult,
                        accum_out=src_dst[:, s, c:c + 1])
                return ins

            def split_target(u, ins):
                ins.then_inc(target_done, 1)
                dve.wait_ge(target_done, u + 1)
                nc.vector.tensor_copy(dst_hi[:, :], src_dst[:, 1, :]).then_inc(dst_hi_done, 1)
                dve.wait_ge(dst_hi_done, u + 1)
                nc.vector.tensor_tensor(dst_lo[:, :], src_dst[:, 1, :], dst_hi[:, :].bitcast(F32),
                                        ALU.subtract).then_inc(dst_done, 1)

            def keep_source(u, ins, bias):
                ins.then_inc(source_done, 1)
                dve.wait_ge(source_done, u + 1)
                nc.vector.tensor_scalar(src_b[:, :], src_dst[:, 0, :], bias, None, ALU.add
                                        ).then_inc(src_done, 1)

            def layer_row(l, name):
                return vec[:, bass.ds(l, 1), VEC.index(name), :].rearrange("p l d -> p (l d)")

            def target_scores(l, u, layer_0=False):
                wait_input(dve, u, layer_0)
                if not (isinstance(u, int) and u == 0):
                    dve.wait_ge(pt_done, u)
                split_target(u, node_products(lambda c: tile_state(u, c), 1,
                                              layer_row(l, "w_dst")))

            def source_scores(l, u):
                keep_source(u, node_products(lambda c: tile_state(u, c), 0,
                                             layer_row(l, "w_src")), ab_col[:, bass.ds(l, 1)])

            def x_low(u):
                dve.wait_ge(x_hi_done, u + 1)
                nc.vector.tensor_tensor(x_lo[:, :, :], unit_state(u), x_hi[:, :, :].bitcast(F32),
                                        ALU.subtract).then_inc(x_split, 1)

            def row_max(u):
                dve.wait_ge(edges_done, u + 1)
                nc.vector.scalar_tensor_tensor(prob[:, :, :], prob[:, :, :], SLOPE, prob[:, :, :],
                                               ALU.mult, ALU.max).then_inc(leaky_done, 1)
                dve.wait_ge(leaky_done, u + 1)
                nc.vector.tensor_reduce(neg_max[:, :], prob[:, :, :], AX.X, ALU.max, negate=True
                                        ).then_inc(max_done, 1)

            def transposed_low(u):
                for b in range(GRAPHS):
                    dve.wait_ge(pt_hi_done, GRAPHS * u + b + 1)
                    nc.vector.tensor_tensor(
                        pt_lo[:, b, :, :].rearrange("p j i -> p (j i)"), t_ps[:, b, :],
                        pt_hi[:, b, :, :].rearrange("p j i -> p (j i)").bitcast(F32),
                        ALU.subtract).then_inc(pt_split, 1)

            def invert(u):
                dve.wait_ge(exp_done, u + 1)
                nc.vector.reciprocal(row_inv[:, :], row_sum[:, :]).then_inc(inv_done, 1)

            def residual1(u):
                dve.wait_ge(agg_done, u + 1)
                dve.wait_ge(inv_done, u + 1)
                if not (isinstance(u, int) and u == 0):
                    dve.wait_ge(h_bias_done, u)
                    dve.wait_ge(ht_done, u)
                for c in range(TILES):
                    ins = nc.vector.scalar_tensor_tensor(h[:, c, :], s_ps[:, c, :],
                                                         row_inv[:, c:c + 1], tile_state(u, c),
                                                         ALU.mult, ALU.add)
                ins.then_inc(res1_done, 1)

            def norm1_stats(u, c0=0, c1=TILES):
                if c0 == 0:
                    wait_alone(dve, res1_done, u + 1)
                return block_stats(lambda c: h[:, c, :], c0, c1)

            def h_low(v):
                for k in range(KB):
                    dve.wait_ge(ht_hi_done, KB * v + k + 1)
                    nc.vector.tensor_tensor(ht_lo[:, k, :], t_ps[:, k, :],
                                            ht_hi[:, k, :].bitcast(F32), ALU.subtract
                                            ).then_inc(ht_split, 1)

            def feed_low(t, f):
                dve.wait_ge(g_hi_done, FB * t + f + 1)
                nc.vector.tensor_tensor(gt_lo[:, f, :], g_raw[:, f % 2, :],
                                        gt_hi[:, f, :].bitcast(F32), ALU.subtract
                                        ).then_inc(g_split, 1)

            def residual2(t, b):
                dve.wait_ge(y_done, 2 * t + b + 1)
                dve.wait_ge(h_bias_done, t + 1)
                rows = state[:, bass.ds(t % GROUPS, 1), 2 * b:2 * b + 2, :].rearrange(
                    "p g c d -> p (g c) d")
                hb = h_bias[:, bass.ds(t % 2, 1), 2 * b:2 * b + 2, :].rearrange(
                    "p s c d -> p (s c) d")
                nc.vector.tensor_tensor(rows, y_ps[:, 2 * b:2 * b + 2, :], hb, ALU.add
                                        ).then_inc(res2_done, 1)

            def norm2_moments(t):
                wait_alone(dve, res2_done, 2 * (t + 1))
                moments(norm2_index(t), lambda c: tile_state(t, c))

            def norm2(t):
                normalise(norm2_index(t), lambda c: tile_state(t, c), lambda c: tile_state(t, c),
                          norm2_done)

            def split_weights(l, chunks):
                for k in chunks:
                    dve.wait_ge(w_hi_done, CHUNKS * l + k + 1)
                    nc.vector.tensor_tensor(weight_chunk(False, k), w_raw[:, k % 2, :],
                                            weight_chunk(True, k).bitcast(F32), ALU.subtract
                                            ).then_inc(w_split, 1)

            def final_moments(d):
                wait_alone(dve, x1_done, d + 1)
                relu_moments(GROUPS + d, lambda c: tile_state(d, c))

            def begin(t, gathers=True):
                feed_low(t, 0)
                if gathers:
                    transposed_low(t + 1)
                    invert(t + 1)
                feed_low(t, 1)
                feed_low(t, 2)

            def complete(t, gathers=True, l_after=None, l_weights=None, attend_0=False,
                         enters=False, final=None):
                feed_low(t, 3)
                if gathers:
                    residual1(t + 1)
                    norm1_stats(t + 1, 0, TILES // 2)
                feed_low(t, 4)
                if gathers:
                    norm1_stats(t + 1, TILES // 2, TILES).then_inc(stats_done, 1)
                feed_low(t, 5)
                if gathers:
                    combine_stats(norm1_index(t + 1))
                feed_low(t, 6)
                feed_low(t, 7)
                if l_after is not None:
                    target_scores(l_after, t + 2, attend_0)
                    source_scores(l_after, t + 2)
                if enters:
                    enter(t + AHEAD)
                if final is not None:
                    final_moments(final)
                if l_weights is not None:
                    split_weights(l_weights, W1_CHUNKS)
                residual2(t, 0)
                if l_after is not None:
                    row_max(t + 2)
                if gathers:
                    h_low(t + 1)
                if enters:
                    enter_mask(t + AHEAD, adj_in_w_raw(t + AHEAD))
                residual2(t, 1)
                if l_after is not None:
                    x_low(t + 2)
                norm2_moments(t)

            dve.wait_ge(ident_set, 4)
            enter(0)
            enter_mask(0, adj_in_h_bias(0))
            dve.wait_ge(vec_loaded, DMA)
            target_scores(0, 0, True)
            source_scores(0, 0)
            enter(1)
            row_max(0)
            x_low(0)
            enter_mask(1, adj_in_h_bias(1))
            enter(2)
            enter_mask(2, adj_in_h_bias(2))
            transposed_low(0)
            invert(0)
            target_scores(0, 1, True)
            source_scores(0, 1)
            split_weights(0, W1_CHUNKS)
            residual1(0)
            norm1_stats(0).then_inc(stats_done, 1)
            combine_stats(norm1_index(0))
            row_max(1)
            x_low(1)
            split_weights(0, W2_CHUNKS)
            h_low(0)
            dve.wait_ge(vec_loaded, 2 * DMA)

            def last_of_layer(l):
                t = l * GROUPS + GROUPS - 1
                complete(t, l_after=l + 1, l_weights=l + 1)
                split_weights(l + 1, W2_CHUNKS)
                begin(t + 1)
                norm2(t)

            begin(0)
            with dve.Fori(0, GROUPS - AHEAD) as t:
                complete(t, l_after=0, attend_0=True, enters=True)
                begin(t + 1)
                norm2(t)
            for t in (GROUPS - 3, GROUPS - 2):
                complete(t, l_after=(t + 2) // GROUPS, attend_0=t + 2 < GROUPS)
                begin(t + 1)
                norm2(t)
            last_of_layer(0)
            with dve.Fori(1, LAYERS - 1) as l:
                with dve.Fori(0, GROUPS - 1) as g:
                    t = l * GROUPS + g
                    complete(t, l_after=(t + 2) // GROUPS)
                    begin(t + 1)
                    norm2(t)
                last_of_layer(l)
            last, t0 = LAYERS - 1, (LAYERS - 1) * GROUPS
            with dve.Fori(0, GROUPS - 2) as g:
                complete(t0 + g, l_after=last)
                begin(t0 + g + 1)
                norm2(t0 + g)
            complete(UNITS - 2, final=0)
            begin(UNITS - 1, gathers=False)

            def project_low(d, p):
                for b in range(2):
                    dve.wait_ge(wh_hi_done, 2 * d + b + 1)
                    ins = nc.vector.tensor_tensor(
                        wh_lo[p][:, 2 * b:2 * b + 2, :], y_ps[:, 2 * b:2 * b + 2, :],
                        wh_hi[p][:, 2 * b:2 * b + 2, :].bitcast(F32), ALU.subtract)
                ins.then_inc(x_split, 1)

            def top_eight(d):
                wait_alone(dve, exp_done, UNITS + d + 1)
                for c in range(TILES):
                    ins = nc.vector.max(top8[:, c, :], prob[:, c, :])
                ins.then_inc(top8_done, 1)
                wait_alone(dve, top8_done, d + 1)
                for c in range(TILES):
                    ins = nc.vector.match_replace(rest[:, c, :], top8[:, c, :], prob[:, c, :], -1.0)
                ins.then_inc(replaced, 1)

            def keep_top(d):
                wait_alone(dve, replaced, d + 1)
                for c in range(TILES):
                    ins = nc.vector.max(next8[:, c, :], rest[:, c, :])
                ins.then_inc(next8_done, 1)
                dve.wait_ge(next8_done, d + 1)
                kth = TOP - 8 - 1
                for c in range(TILES):
                    ins = nc.vector.scalar_tensor_tensor(prob[:, c, :], prob[:, c, :],
                                                         next8[:, c, kth:kth + 1], prob[:, c, :],
                                                         ALU.is_ge, ALU.mult)
                ins.then_inc(kept_done, 1)

            rest = g_raw[:, :, :].rearrange("p s (c n) -> p (s c) n", n=N)
            dve.wait_ge(wo_hi_done, 1)
            nc.vector.tensor_tensor(wo_lo, wo_raw, wo_hi.bitcast(F32), ALU.subtract
                                    ).then_inc(wo_split, 1)
            dve.wait_ge(pt_done, UNITS)
            for i in range(2 * KB):
                part, k = i // KB, i % KB
                ins = nc.vector.scalar_tensor_tensor(
                    prob_unused[:, k, part, :], wo_raw[:, k, :], 1.0, vec[:, 0, part, :],
                    ALU.mult, ALU.mult, accum_out=wa[:, i:i + 1])
            ins.then_inc(wa_done, 1)
            dve.wait_ge(wa_done, 1)
            nc.vector.tensor_copy(wa_hi[:, :], wa).then_inc(wa_hi_done, 1)
            dve.wait_ge(wa_hi_done, 1)
            nc.vector.tensor_tensor(wa_lo[:, :], wa, wa_hi[:, :].bitcast(F32), ALU.subtract
                                    ).then_inc(wa_split, 1)
            norm2(UNITS - 2)
            for f in range(3, FB):
                feed_low(UNITS - 1, f)
            final_moments(1)
            h_low(UNITS)
            residual2(UNITS - 1, 0)
            residual2(UNITS - 1, 1)
            norm2_moments(UNITS - 1)
            norm2(UNITS - 1)
            project_low(0, 0)

            def final_step(k, p):
                u = UNITS + k
                more = not (isinstance(k, int) and k == GROUPS - 1)
                row_max(u)
                if more:
                    h_low(u + 1)
                if not (isinstance(k, int) and k + 2 >= GROUPS):
                    final_moments(k + 2)
                top_eight(k)
                keep_top(k)
                if more:
                    project_low(k + 1, 1 - p)
                transposed_low(u)
                if not (isinstance(k, int) and k == 0):
                    dve.wait_ge(elu_done, k)
                invert(u)
                dve.wait_ge(inv_done, u + 1)
                nc.vector.tensor_scalar(neg_inv[:, :], row_inv[:, :], -1.0, None, ALU.mult
                                        ).then_inc(neg_inv_done, 1)

            final_steps(dve, final_step)


def kernel(**inputs):
    import numpy as np
    import concourse.bacc as bacc
    from concourse import mybir as mb
    from concourse.bass_utils import run_bass_kernel_spmd

    get = {k: np.ascontiguousarray(v) for k, v in inputs.items()}
    layers, d2 = get["L0_gnn_attn_w"].shape
    d = d2 // 2
    w = get["L0_gnn_attn_w"]
    vectors = np.stack([w[:, :d], w[:, d:], get["L0_gnn_g1"], get["L0_gnn_beta1"], get["L0_gnn_b2"],
                        get["L0_gnn_g2"], get["L0_gnn_beta2"]], axis=1).reshape(-1)
    b1 = get["L0_gnn_b1"]
    b1_cols = b1.reshape(layers, -1, 128).transpose(2, 0, 1).reshape(128, -1)
    eye = np.eye(128, dtype=np.float32)
    arrays = {
        "x": get["x"], "adj": get["adj"], "vectors": vectors, "attn_b": get["L0_gnn_attn_b"],
        "w1": get["L0_gnn_W1"], "b1": b1_cols, "w2": get["L0_gnn_W2"], "w_out": get["L1_gnn_W"],
        "a_out": get["L1_gnn_a"].reshape(-1),
        "diagonals": np.concatenate([eye, eye * np.float32(-9e15)], axis=1),
    }
    nc = bacc.Bacc("TRN2", target_bir_lowering=False, num_devices=1)
    arrays = {f"in_{k}": np.ascontiguousarray(v) for k, v in arrays.items()}
    args = [nc.dram_tensor(k, a.shape, mb.dt.from_np(a.dtype), kind="ExternalInput").ap()
            for k, a in arrays.items()]
    out = nc.dram_tensor("out_x", get["x"].shape, mb.dt.float32, kind="ExternalOutput").ap()
    gnn_adjacency_kernel(nc, *args, out)
    r = run_bass_kernel_spmd(nc, [arrays], core_ids=[0])
    return r.results[0]["out_x"]
```
